# Optimizing a Trainium2 kernel written in Bass

```python
import numpy as np
import jax
import jax.numpy as jnp

def _softmax(x, axis=-1):
    return jax.nn.softmax(x, axis=axis)

def _gelu(x):
    return jax.nn.gelu(x, approximate=True)

def _silu(x):
    return jax.nn.silu(x)

def _sigmoid(x):
    return jax.nn.sigmoid(x)

def _layernorm(x, axis=-1, eps=1e-05):
    m = jnp.mean(x, axis=axis, keepdims=True)
    v = jnp.var(x, axis=axis, keepdims=True)
    return (x - m) / jnp.sqrt(v + eps)

def _scatter_add(tgt, idx, src, axis=0):
    return tgt.at[idx].add(src)

def _segment_sum(src, seg, n):
    return jax.ops.segment_sum(src, seg, n)
kernel_name = 'mk_conv_seq_d4_conv_nchw256_r2_d023ee'

def setup_inputs(seed: int=0):
    np.random.seed(seed)
    _w = jnp.asarray

    def _rec_inputs():
        import jax
        import jax.numpy as jnp
        _gk = jax.random.key(seed)
        x = -0.0002928 + 1 * jax.random.normal(jax.random.fold_in(_gk, 1), (4, 128, 32, 32), jnp.float32)
        return x
    x = _rec_inputs()

    def _L0_conv_setup():
        import jax, jax.numpy as jnp
        import numpy as np
        B, C, H, W, S = (4, 128, 32, 32, 8)
        key = jax.random.key(seed)
        k1, k2, k3 = jax.random.split(key, 3)
        x = jax.random.normal(k1, (B, C, H, W), dtype=jnp.float32)
        w_conv = jax.random.normal(k2, (S * S, C), dtype=jnp.float32) * 0.05
        w_gap = jax.random.normal(k3, (C, C), dtype=jnp.float32) * 0.05
        return {'x': x, 'w_conv': w_conv, 'w_gap': w_gap}
    _L0_conv_all = _L0_conv_setup()
    _L0_conv_in = {k: v for k, v in _L0_conv_all.items() if k in ('w_conv', 'w_gap')}
    del _L0_conv_all

    def _L1_conv_setup():
        import jax, jax.numpy as jnp
        import numpy as np
        B, C, H, W = (4, 128, 32, 32)
        CQK = C // 8
        EPS = 1e-05

        def _make_proj(key, c_out, c_in):
            kw, km = jax.random.split(key)
            w = jax.random.normal(kw, (c_out, c_in), jnp.float32) * (1.0 / np.sqrt(c_in))
            b = jnp.zeros((c_out,), jnp.float32)
            bn_g = jnp.ones((c_out,), jnp.float32)
            bn_b = jnp.zeros((c_out,), jnp.float32)
            bn_mean = jax.random.normal(km, (c_out,), jnp.float32) * 0.1
            bn_var = jnp.ones((c_out,), jnp.float32) * 0.9
            return (w, b, bn_g, bn_b, bn_mean, bn_var)

        def _conv1x1_bn(xf, w, b, g, beta, mean, var):
            y = jnp.einsum('oc,bcn->bon', w, xf) + b[None, :, None]
            scale = (g * jax.lax.rsqrt(var + EPS))[None, :, None]
            shift = (beta - mean * g * jax.lax.rsqrt(var + EPS))[None, :, None]
            return y * scale + shift
        key = jax.random.key(seed)
        kx, kq, kk, kv = jax.random.split(key, 4)
        x = jax.random.normal(kx, (B, C, H, W), jnp.float32)
        q_w, q_b, q_g, q_beta, q_mean, q_var = _make_proj(kq, CQK, C)
        k_w, k_b, k_g, k_beta, k_mean, k_var = _make_proj(kk, CQK, C)
        v_w, v_b, v_g, v_beta, v_mean, v_var = _make_proj(kv, C, C)
        gamma = jnp.array([0.5], jnp.float32)
        return dict(x=x, q_w=q_w, q_b=q_b, q_g=q_g, q_beta=q_beta, q_mean=q_mean, q_var=q_var, k_w=k_w, k_b=k_b, k_g=k_g, k_beta=k_beta, k_mean=k_mean, k_var=k_var, v_w=v_w, v_b=v_b, v_g=v_g, v_beta=v_beta, v_mean=v_mean, v_var=v_var, gamma=gamma)
    _L1_conv_all = _L1_conv_setup()
    _L1_conv_in = {k: v for k, v in _L1_conv_all.items() if k in ('q_w', 'q_b', 'q_g', 'q_beta', 'q_mean', 'q_var', 'k_w', 'k_b', 'k_g', 'k_beta', 'k_mean', 'k_var', 'v_w', 'v_b', 'v_g', 'v_beta', 'v_mean', 'v_var', 'gamma')}
    del _L1_conv_all

    def _L2_conv_setup():
        import jax, jax.numpy as jnp
        import numpy as np
        B, C, H, W = (16, 128, 32, 32)
        HID = C // 8
        NEG = -9000000000000000.0

        def _spatial_adj(h, w):
            ii, jj = np.meshgrid(np.arange(h), np.arange(w), indexing='ij')
            pi, pj = (ii.reshape(-1), jj.reshape(-1))
            di = np.abs(pi[:, None] - pi[None, :])
            dj = np.abs(pj[:, None] - pj[None, :])
            return (di <= 1) & (dj <= 1) & ~((di == 0) & (dj == 0))

        def _channel_adj(c):
            i = np.arange(c)
            return np.abs(i[:, None] - i[None, :]) == 1

        def _bn_relu(y, g, b, m, v):
            inv = g / jnp.sqrt(v + 1e-05)
            return jax.nn.relu(y * inv[:, None, None] + (b - m * inv)[:, None, None])
        key = jax.random.key(seed)
        ks = jax.random.split(key, 12)
        return {'x': jax.random.normal(ks[0], (B, C, H, W), dtype=jnp.float32), 'wa': jax.random.normal(ks[1], (HID, C), dtype=jnp.float32) * 0.05, 'ga': jax.random.uniform(ks[2], (HID,), dtype=jnp.float32) + 0.5, 'ba': jax.random.normal(ks[3], (HID,), dtype=jnp.float32) * 0.1, 'ma': jnp.zeros((HID,), dtype=jnp.float32), 'va': jnp.ones((HID,), dtype=jnp.float32), 'ws': jax.random.normal(ks[4], (HID, C), dtype=jnp.float32) * 0.05, 'gs': jax.random.uniform(ks[5], (HID,), dtype=jnp.float32) + 0.5, 'bs': jax.random.normal(ks[6], (HID,), dtype=jnp.float32) * 0.1, 'ms': jnp.zeros((HID,), dtype=jnp.float32), 'vs': jnp.ones((HID,), dtype=jnp.float32), 'gama': jax.random.uniform(ks[7], (1,), dtype=jnp.float32)}
    _L2_conv_all = _L2_conv_setup()
    _L2_conv_in = {k: v for k, v in _L2_conv_all.items() if k in ('wa', 'ga', 'ba', 'ma', 'va', 'ws', 'gs', 'bs', 'ms', 'vs', 'gama')}
    del _L2_conv_all

    def _L3_conv_setup():
        import math
        import jax, jax.numpy as jnp
        import numpy as np
        STRATEGY = 'small'
        K_PEAKS = 2
        BW = math.radians(15.0)
        HIGH_RATIO = 0.3
        LOW_RATIO = 0.2
        ALPHA = 1.2
        BETA = 0.8
        N_BINS = 90

        def _forward(x, w_in, w_out):
            B, C, H, W = x.shape
            pi = jnp.float32(math.pi)
            cy, cx = (H // 2, W // 2)
            y = jnp.arange(H, dtype=jnp.float32)[:, None]
            xg = jnp.arange(W, dtype=jnp.float32)[None, :]
            r = jnp.sqrt((y - cy) ** 2 + (xg - cx) ** 2)
            theta = jnp.arctan2(y - cy, xg - cx) + pi
            r_max = float(min(cy, cx))
            x_proj = jnp.einsum('mc,bchw->bmhw', w_in, x)
            fs = jnp.fft.fftshift(jnp.fft.fft2(x_proj, norm='ortho'), axes=(-2, -1))
            mag = jnp.abs(fs)
            theta_mod = theta % pi
            high_mask = (r > HIGH_RATIO * r_max).astype(jnp.float32)
            bin_edges = jnp.linspace(0.0, math.pi, N_BINS + 1, dtype=jnp.float32)
            mag_avg = mag.mean(axis=1)
            weighted = (mag_avg * high_mask).reshape(B, -1)
            bin_idx = jnp.clip(jnp.searchsorted(bin_edges, theta_mod.reshape(-1), side='left') - 1, 0, N_BINS - 1)
            energy = jax.vmap(lambda w: jax.ops.segment_sum(w, bin_idx, num_segments=N_BINS))(weighted)
            ep = jnp.pad(energy, ((0, 0), (1, 1)))
            es = 0.25 * ep[:, :-2] + 0.5 * ep[:, 1:-1] + 0.25 * ep[:, 2:]
            mean_e = es.mean(axis=-1, keepdims=True)
            is_peak = (es > mean_e) & (es > jnp.roll(es, 1, axis=-1)) & (es > jnp.roll(es, -1, axis=-1))
            vals = jnp.where(is_peak, es, -jnp.inf)
            topv, topi = jax.lax.top_k(vals, K_PEAKS)
            count = jnp.sum(topv > -jnp.inf, axis=-1)
            amax = jnp.argmax(es, axis=-1)
            topi = jnp.where((count > 0)[:, None], topi, amax[:, None])
            eff = jnp.maximum(count, 1)
            pos = jnp.minimum(jnp.arange(K_PEAKS)[None, :], (eff - 1)[:, None])
            final_idx = jnp.take_along_axis(topi, pos, axis=1)
            bin_center = (bin_edges[:-1] + bin_edges[1:]) * 0.5
            peak_angles = bin_center[final_idx]
            if STRATEGY == 'small':
                pa = peak_angles
                base_mask = high_mask
            else:
                pa = (peak_angles + pi / 2) % pi
                base_mask = (r <= LOW_RATIO * r_max).astype(jnp.float32)
            diff = jnp.abs(theta[None, None] - pa[:, :, None, None])
            diff = jnp.minimum(diff, pi - diff)
            in_region = (diff <= BW) & (base_mask[None, None] > 0)
            enh = jnp.any(in_region, axis=1).astype(jnp.float32)
            gain = jnp.where(enh > 0, jnp.float32(ALPHA), jnp.float32(1.0))
            other_high = high_mask[None] * (1.0 - enh)
            gain = gain * (1.0 - other_high) + other_high * BETA
            fs_enh = fs * gain[:, None, :, :]
            x_enh = jnp.fft.ifft2(jnp.fft.ifftshift(fs_enh, axes=(-2, -1)), norm='ortho').real
            out = jnp.einsum('cm,bmhw->bchw', w_out, x_enh)
            return x + out
        key = jax.random.key(seed)
        k1, k2, k3 = jax.random.split(key, 3)
        x = jax.random.normal(k1, (16, 128, 64, 64), dtype=jnp.float32)
        w_in = jax.random.normal(k2, (16, 128), dtype=jnp.float32) * 0.06
        w_out = jax.random.normal(k3, (128, 16), dtype=jnp.float32) * 0.25
        return {'x': x, 'w_in': w_in, 'w_out': w_out}
    _L3_conv_all = _L3_conv_setup()
    _L3_conv_in = {k: v for k, v in _L3_conv_all.items() if k in ('w_in', 'w_out')}
    del _L3_conv_all
    return {'x': x, 'L0_conv_w_conv': _L0_conv_in['w_conv'], 'L0_conv_w_gap': _L0_conv_in['w_gap'], 'L1_conv_q_w': _L1_conv_in['q_w'], 'L1_conv_q_b': _L1_conv_in['q_b'], 'L1_conv_q_g': _L1_conv_in['q_g'], 'L1_conv_q_beta': _L1_conv_in['q_beta'], 'L1_conv_q_mean': _L1_conv_in['q_mean'], 'L1_conv_q_var': _L1_conv_in['q_var'], 'L1_conv_k_w': _L1_conv_in['k_w'], 'L1_conv_k_b': _L1_conv_in['k_b'], 'L1_conv_k_g': _L1_conv_in['k_g'], 'L1_conv_k_beta': _L1_conv_in['k_beta'], 'L1_conv_k_mean': _L1_conv_in['k_mean'], 'L1_conv_k_var': _L1_conv_in['k_var'], 'L1_conv_v_w': _L1_conv_in['v_w'], 'L1_conv_v_b': _L1_conv_in['v_b'], 'L1_conv_v_g': _L1_conv_in['v_g'], 'L1_conv_v_beta': _L1_conv_in['v_beta'], 'L1_conv_v_mean': _L1_conv_in['v_mean'], 'L1_conv_v_var': _L1_conv_in['v_var'], 'L1_conv_gamma': _L1_conv_in['gamma'], 'L2_conv_wa': _L2_conv_in['wa'], 'L2_conv_ga': _L2_conv_in['ga'], 'L2_conv_ba': _L2_conv_in['ba'], 'L2_conv_ma': _L2_conv_in['ma'], 'L2_conv_va': _L2_conv_in['va'], 'L2_conv_ws': _L2_conv_in['ws'], 'L2_conv_gs': _L2_conv_in['gs'], 'L2_conv_bs': _L2_conv_in['bs'], 'L2_conv_ms': _L2_conv_in['ms'], 'L2_conv_vs': _L2_conv_in['vs'], 'L2_conv_gama': _L2_conv_in['gama'], 'L3_conv_w_in': _L3_conv_in['w_in'], 'L3_conv_w_out': _L3_conv_in['w_out']}

def reference(x, L0_conv_w_conv, L0_conv_w_gap, L1_conv_q_w, L1_conv_q_b, L1_conv_q_g, L1_conv_q_beta, L1_conv_q_mean, L1_conv_q_var, L1_conv_k_w, L1_conv_k_b, L1_conv_k_g, L1_conv_k_beta, L1_conv_k_mean, L1_conv_k_var, L1_conv_v_w, L1_conv_v_b, L1_conv_v_g, L1_conv_v_beta, L1_conv_v_mean, L1_conv_v_var, L1_conv_gamma, L2_conv_wa, L2_conv_ga, L2_conv_ba, L2_conv_ma, L2_conv_va, L2_conv_ws, L2_conv_gs, L2_conv_bs, L2_conv_ms, L2_conv_vs, L2_conv_gama, L3_conv_w_in, L3_conv_w_out):
    import jax
    import jax.numpy as jnp

    def _L0_conv_ref(x, w_conv, w_gap):
        import jax, jax.numpy as jnp
        import numpy as np
        B, C, H, W, S = (4, 128, 32, 32, 8)
        b, c, h, w = x.shape
        hw = h * w
        xr = x.reshape(b, c, hw)
        mm1 = jax.nn.softmax(jnp.einsum('bci,bcj->bij', xr, xr), axis=-1)
        x_conv = jnp.einsum('oc,bci->boi', w_conv, xr)
        mm2 = jnp.einsum('boi,bij->boj', x_conv, mm1)
        gap = x.reshape(b, c, S, h // S, S, w // S).mean(axis=(3, 5))
        gap = jax.nn.relu(jnp.einsum('oc,bcst->bost', w_gap, gap))
        gap = gap.reshape(b, c, S * S)
        mm3 = jnp.einsum('bcs,bsj->bcj', gap, mm2).reshape(b, c, h, w)
        return mm3 + x

    def _L1_conv_ref(x, q_w, q_b, q_g, q_beta, q_mean, q_var, k_w, k_b, k_g, k_beta, k_mean, k_var, v_w, v_b, v_g, v_beta, v_mean, v_var, gamma):
        import jax, jax.numpy as jnp
        import numpy as np
        B, C, H, W = (4, 128, 32, 32)
        CQK = C // 8
        EPS = 1e-05

        def _make_proj(key, c_out, c_in):
            kw, km = jax.random.split(key)
            w = jax.random.normal(kw, (c_out, c_in), jnp.float32) * (1.0 / np.sqrt(c_in))
            b = jnp.zeros((c_out,), jnp.float32)
            bn_g = jnp.ones((c_out,), jnp.float32)
            bn_b = jnp.zeros((c_out,), jnp.float32)
            bn_mean = jax.random.normal(km, (c_out,), jnp.float32) * 0.1
            bn_var = jnp.ones((c_out,), jnp.float32) * 0.9
            return (w, b, bn_g, bn_b, bn_mean, bn_var)

        def _conv1x1_bn(xf, w, b, g, beta, mean, var):
            y = jnp.einsum('oc,bcn->bon', w, xf) + b[None, :, None]
            scale = (g * jax.lax.rsqrt(var + EPS))[None, :, None]
            shift = (beta - mean * g * jax.lax.rsqrt(var + EPS))[None, :, None]
            return y * scale + shift
        b_, c_, h_, w_ = x.shape
        n = h_ * w_
        xf = x.reshape(b_, c_, n)
        q = _conv1x1_bn(xf, q_w, q_b, q_g, q_beta, q_mean, q_var)
        k = _conv1x1_bn(xf, k_w, k_b, k_g, k_beta, k_mean, k_var)
        v = _conv1x1_bn(xf, v_w, v_b, v_g, v_beta, v_mean, v_var)
        attn = jax.nn.softmax(jnp.einsum('bci,bcj->bij', q, k), axis=-1)
        out = jnp.einsum('bcj,bij->bci', v, attn).reshape(b_, c_, h_, w_)
        return gamma[0] * out + x

    def _L2_conv_ref(x, wa, ga, ba, ma, va, ws, gs, bs, ms, vs, gama):
        import jax, jax.numpy as jnp
        import numpy as np
        B, C, H, W = (16, 128, 32, 32)
        HID = C // 8
        NEG = -9000000000000000.0

        def _spatial_adj(h, w):
            ii, jj = np.meshgrid(np.arange(h), np.arange(w), indexing='ij')
            pi, pj = (ii.reshape(-1), jj.reshape(-1))
            di = np.abs(pi[:, None] - pi[None, :])
            dj = np.abs(pj[:, None] - pj[None, :])
            return (di <= 1) & (dj <= 1) & ~((di == 0) & (dj == 0))

        def _channel_adj(c):
            i = np.arange(c)
            return np.abs(i[:, None] - i[None, :]) == 1

        def _bn_relu(y, g, b, m, v):
            inv = g / jnp.sqrt(v + 1e-05)
            return jax.nn.relu(y * inv[:, None, None] + (b - m * inv)[:, None, None])
        b, c, h, w = x.shape
        n = h * w
        adj = jnp.asarray(_spatial_adj(h, w))
        cadj = jnp.asarray(_channel_adj(c))
        alpha = _bn_relu(jnp.einsum('bchw,oc->bohw', x, wa), ga, ba, ma, va)
        sigma = _bn_relu(jnp.einsum('bchw,oc->bohw', x, ws), gs, bs, ms, vs)
        xf = x.reshape(b, c, n)
        af = alpha.reshape(b, -1, n)
        sf = sigma.reshape(b, -1, n)
        att = jnp.einsum('bkn,bkm->bnm', af, sf)
        att = jax.nn.softmax(jnp.where(adj, att, NEG), axis=2)
        h_s = jnp.einsum('bnm,bcm->bcn', att, xf).reshape(b, c, h, w)
        Gc = jnp.einsum('bcn,bdn->bcd', xf, xf)
        catt = jax.nn.softmax(jnp.where(cadj, Gc, NEG), axis=2)
        h_p = jnp.einsum('bcd,bdn->bcn', catt, xf).reshape(b, c, h, w)
        h_prime = jax.nn.elu(h_s + h_p)
        return (1.0 - gama) * x + gama * h_prime

    def _L3_conv_ref(x, w_in, w_out):
        import math
        import jax, jax.numpy as jnp
        import numpy as np
        STRATEGY = 'small'
        K_PEAKS = 2
        BW = math.radians(15.0)
        HIGH_RATIO = 0.3
        LOW_RATIO = 0.2
        ALPHA = 1.2
        BETA = 0.8
        N_BINS = 90

        def _forward(x, w_in, w_out):
            B, C, H, W = x.shape
            pi = jnp.float32(math.pi)
            cy, cx = (H // 2, W // 2)
            y = jnp.arange(H, dtype=jnp.float32)[:, None]
            xg = jnp.arange(W, dtype=jnp.float32)[None, :]
            r = jnp.sqrt((y - cy) ** 2 + (xg - cx) ** 2)
            theta = jnp.arctan2(y - cy, xg - cx) + pi
            r_max = float(min(cy, cx))
            x_proj = jnp.einsum('mc,bchw->bmhw', w_in, x)
            fs = jnp.fft.fftshift(jnp.fft.fft2(x_proj, norm='ortho'), axes=(-2, -1))
            mag = jnp.abs(fs)
            theta_mod = theta % pi
            high_mask = (r > HIGH_RATIO * r_max).astype(jnp.float32)
            bin_edges = jnp.linspace(0.0, math.pi, N_BINS + 1, dtype=jnp.float32)
            mag_avg = mag.mean(axis=1)
            weighted = (mag_avg * high_mask).reshape(B, -1)
            bin_idx = jnp.clip(jnp.searchsorted(bin_edges, theta_mod.reshape(-1), side='left') - 1, 0, N_BINS - 1)
            energy = jax.vmap(lambda w: jax.ops.segment_sum(w, bin_idx, num_segments=N_BINS))(weighted)
            ep = jnp.pad(energy, ((0, 0), (1, 1)))
            es = 0.25 * ep[:, :-2] + 0.5 * ep[:, 1:-1] + 0.25 * ep[:, 2:]
            mean_e = es.mean(axis=-1, keepdims=True)
            is_peak = (es > mean_e) & (es > jnp.roll(es, 1, axis=-1)) & (es > jnp.roll(es, -1, axis=-1))
            vals = jnp.where(is_peak, es, -jnp.inf)
            topv, topi = jax.lax.top_k(vals, K_PEAKS)
            count = jnp.sum(topv > -jnp.inf, axis=-1)
            amax = jnp.argmax(es, axis=-1)
            topi = jnp.where((count > 0)[:, None], topi, amax[:, None])
            eff = jnp.maximum(count, 1)
            pos = jnp.minimum(jnp.arange(K_PEAKS)[None, :], (eff - 1)[:, None])
            final_idx = jnp.take_along_axis(topi, pos, axis=1)
            bin_center = (bin_edges[:-1] + bin_edges[1:]) * 0.5
            peak_angles = bin_center[final_idx]
            if STRATEGY == 'small':
                pa = peak_angles
                base_mask = high_mask
            else:
                pa = (peak_angles + pi / 2) % pi
                base_mask = (r <= LOW_RATIO * r_max).astype(jnp.float32)
            diff = jnp.abs(theta[None, None] - pa[:, :, None, None])
            diff = jnp.minimum(diff, pi - diff)
            in_region = (diff <= BW) & (base_mask[None, None] > 0)
            enh = jnp.any(in_region, axis=1).astype(jnp.float32)
            gain = jnp.where(enh > 0, jnp.float32(ALPHA), jnp.float32(1.0))
            other_high = high_mask[None] * (1.0 - enh)
            gain = gain * (1.0 - other_high) + other_high * BETA
            fs_enh = fs * gain[:, None, :, :]
            x_enh = jnp.fft.ifft2(jnp.fft.ifftshift(fs_enh, axes=(-2, -1)), norm='ortho').real
            out = jnp.einsum('cm,bmhw->bchw', w_out, x_enh)
            return x + out
        return _forward(x, w_in, w_out)

    def _gn(v, G=32, eps=1e-05):
        B_, C_, H_, W_ = v.shape
        g = v.reshape(B_, G, C_ // G, H_, W_)
        m = jnp.mean(g, axis=(2, 3, 4), keepdims=True)
        s = jnp.var(g, axis=(2, 3, 4), keepdims=True)
        return ((g - m) / jnp.sqrt(s + eps)).reshape(v.shape)

    def _ln_c(v, eps=1e-06):
        m = jnp.mean(v, axis=1, keepdims=True)
        s = jnp.var(v, axis=1, keepdims=True)
        return (v - m) / jnp.sqrt(s + eps)

    def _ln_t(v, eps=1e-05):
        m = jnp.mean(v, axis=-1, keepdims=True)
        s = jnp.var(v, axis=-1, keepdims=True)
        return (v - m) / jnp.sqrt(s + eps)

    def _to_tokens(v):
        B_, C_, H_, W_ = v.shape
        return v.reshape(B_, C_, H_ * W_).transpose(0, 2, 1)

    def _from_tokens(t, like):
        B_, C_, H_, W_ = like.shape
        return t.transpose(0, 2, 1).reshape(B_, C_, H_, W_)
    x = _L0_conv_ref(x, L0_conv_w_conv, L0_conv_w_gap)
    x = _L1_conv_ref(x, L1_conv_q_w, L1_conv_q_b, L1_conv_q_g, L1_conv_q_beta, L1_conv_q_mean, L1_conv_q_var, L1_conv_k_w, L1_conv_k_b, L1_conv_k_g, L1_conv_k_beta, L1_conv_k_mean, L1_conv_k_var, L1_conv_v_w, L1_conv_v_b, L1_conv_v_g, L1_conv_v_beta, L1_conv_v_mean, L1_conv_v_var, L1_conv_gamma)
    x = _L2_conv_ref(x, L2_conv_wa, L2_conv_ga, L2_conv_ba, L2_conv_ma, L2_conv_va, L2_conv_ws, L2_conv_gs, L2_conv_bs, L2_conv_ms, L2_conv_vs, L2_conv_gama)
    x = _L3_conv_ref(x, L3_conv_w_in, L3_conv_w_out)
    return x

_drawn_inputs = setup_inputs


def setup_inputs(seed=0):
    import zlib

    import numpy as np

    out = dict(_drawn_inputs(seed))
    spreads = {'L1_conv_q_b': (0.0, 0.1),
     'L1_conv_q_g': (1.0, 0.2),
     'L1_conv_q_beta': (0.0, 0.1),
     'L1_conv_q_var': (0.8999999761581421, 0.2),
     'L1_conv_k_b': (0.0, 0.8),
     'L1_conv_k_g': (1.0, 0.2),
     'L1_conv_k_beta': (0.0, 0.8),
     'L1_conv_k_var': (0.8999999761581421, 0.2),
     'L1_conv_v_b': (0.0, 0.1),
     'L1_conv_v_g': (1.0, 0.2),
     'L1_conv_v_beta': (0.0, 0.1),
     'L1_conv_v_var': (0.8999999761581421, 0.2),
     'L2_conv_ma': (0.0, 0.1),
     'L2_conv_va': (1.0, 0.6),
     'L2_conv_ms': (0.0, 0.376),
     'L2_conv_vs': (1.0, 0.6)}
    factors = {'L1_conv_k_mean': 8.0, 'L2_conv_bs': 3.123}
    for name, (base, spread) in spreads.items():
        noise = np.random.default_rng([zlib.crc32(name.encode()), seed]).standard_normal(out[name].shape)
        drawn = base * np.exp(spread * noise) if base else spread * noise
        out[name] = jnp.asarray(drawn.astype(out[name].dtype))
    for name, factor in factors.items():
        out[name] = (out[name] * factor).astype(out[name].dtype)
    return out
```

```python
from contextlib import ExitStack

import numpy as np
import concourse.bass as bass
from concourse import mybir

ALU = mybir.AluOpType
ACT = mybir.ActivationFunctionType
AX = mybir.AxisListType
F32 = mybir.dt.float32
F32R = mybir.dt.float32r
BF16 = mybir.dt.bfloat16

P = 128
B, C, H, W = 4, 128, 32, 32
N = H * W
HALF = N // 2
CH = N // P
POOL = 8
HID = C // 8
G = 32
KS3 = 3 * G
WIN = P + 2 * W
WPAD = 256
M = 16
BM = B * M
NBINS = 90
EPS = 1e-5
Q, K, A_, S_, V = range(5)
RING = 3

L0_HEAD = [("split", 0), ("gap", 0), ("gate", 0), ("val0", 0)]


def l0_chunk(i):
    s = [("gram", i)]
    if i >= 1:
        s += [("norm0", i - 1), ("mix", i - 1)]
    return s


L0_CHUNKS = [l0_chunk(i) for i in range(CH)]
L0_TAIL = [("norm0", CH - 1), ("mix", CH - 1), ("x1", 0)]
L0_ALL = L0_HEAD + sum(L0_CHUNKS, []) + L0_TAIL

SCORES = [[("score", i)] for i in range(CH)]
ATTEND = [[("scoreT", j)] + ([("attend", j - 1)] if j else []) for j in range(CH)]
L1_HEAD = [("qproj", 0), ("kproj", 0), ("val1", 0)]
L2_HEAD = [("aproj", 0), ("sproj", 0), ("x2T", 0)]
L2_MID = [[("near", 0)], [("near", 1)], [("chan", 0)], [("shift2", 0)], [("chanT", 0)],
          [("nearT", 0)], [("nearT", 1)], [("xkeep", 0), ("join", 0)]]
L2_TAIL = [("x3", 0), ("xproj", 0)]

L12_ALL = (L1_HEAD + sum(SCORES, []) + [("shift1", 0)] + sum(ATTEND, [])
           + [("attend", CH - 1), ("x2", 0)] + L2_HEAD + sum(L2_MID, []) + L2_TAIL)


def steady():
    s = L1_HEAD + L0_HEAD
    for i in range(CH):
        s = s + SCORES[i] + (L0_CHUNKS[i // 2] if i % 2 == 0 else [])
    s = s + [("shift1", 0)] + L0_CHUNKS[4]
    for j in range(CH):
        s = s + ATTEND[j]
    s = s + [("attend", CH - 1), ("x2", 0)] + L0_CHUNKS[5] + L2_HEAD
    rest = [[("near", 0), ("near", 1)], [("chan", 0)], L0_CHUNKS[6], [("shift2", 0), ("chanT", 0)],
            L0_CHUNKS[7], [("nearT", 0), ("nearT", 1)], L0_TAIL[:2], [("xkeep", 0), ("join", 0)], L0_TAIL[2:], L2_TAIL]
    return s + sum(rest, [])


STEADY = steady()
USES_TILE = {"gap", "gate", "val0", "gram", "qproj", "kproj", "val1", "score", "shift1", "scoreT",
             "aproj", "sproj", "x2T", "near", "chan", "shift2", "chanT", "nearT", "xproj"}


def tiles_of(schedule):
    return {s: n for n, s in enumerate(x for x in schedule if x[0] in USES_TILE)}


T_FIRST, T_STEADY, T_LAST = tiles_of(L0_ALL), tiles_of(STEADY), tiles_of(L12_ALL)


LAST_READER = {"gap": ("gapT_ready", "a", 1, lambda i: 1), "gate": ("gate_ready", "a", 1, lambda i: 1),
               "val0": ("v0_ready", "a", 1, lambda i: 1), "gram": ("e0_ready", "a", CH, lambda i: i + 1),
               "qproj": ("q_ready", "b", 1, lambda i: 1), "kproj": ("k_ready", "b", 1, lambda i: 1),
               "val1": ("v1_ready", "b", 1, lambda i: 1), "score": ("sum1_ready", "b", 2 * CH, lambda i: i + 1),
               "shift1": ("qs2_ready", "b", 2, lambda i: 1), "shift2": ("qs2_ready", "b", 2, lambda i: 2),
               "scoreT": ("e1_ready", "b", CH, lambda i: i + 1), "aproj": ("full_ready", "b", 2, lambda i: 1),
               "sproj": ("full_ready", "b", 2, lambda i: 2), "x2T": ("x2T_ready", "b", 1, lambda i: 1),
               "chan": ("ec_ready", "b", 1, lambda i: 1), "chanT": ("ecT_ready", "b", 1, lambda i: 1),
               "near": ("sum1_ready", "b", 2 * CH, lambda i: CH + 4 * i + 4),
               "nearT": ("e2_ready", "b", 2, lambda i: i + 1), "xproj": ("xp_ready", "b", 1, lambda i: 1)}


class Phase:

    def __init__(self, schedule, tiles, a, b, base, turn, per_turn, before=None):
        self.schedule, self.tiles, self.a, self.b = schedule, tiles, a, b
        self.base, self.turn, self.per_turn, self.before = base, turn, per_turn, before

    def freed(self, step):
        n = self.tiles[step] - 2
        a, b = self.a, self.b
        order = list(self.tiles)
        if n < 0:
            if self.before is None:
                return None, 0
            order = list(self.before)
            a = self.b if self.a is None else self.a - 1
            b = None if self.b is None else self.b - 1
        name, i = order[n]
        sem, which, per_image, at = LAST_READER[name]
        return sem, (a if which == "a" else b) * per_image + at(i)

    def slot(self, step):
        return (self.base + self.tiles[step]) % 2

    def used(self, step):
        return self.turn * (self.per_turn // 2) + (self.base + self.tiles[step]) // 2


def phases(engine):
    n1, n2 = len(T_FIRST), len(T_STEADY)
    assert n2 % 2 == 0
    yield Phase(L0_ALL, T_FIRST, 0, None, 0, 0, 0)
    yield Phase(STEADY, T_STEADY, 1, 0, n1, 0, n2, T_FIRST)
    with engine.Fori(1, B - 1) as t:
        yield Phase(STEADY, T_STEADY, t + 1, t, n1, t, n2, T_STEADY)
    yield Phase(L12_ALL, T_LAST, None, B - 1, n1 + n2 * (B - 1), 0, 0, T_STEADY)


def wait_past(engine, sem, count):
    if not (isinstance(count, int) and count <= 0):
        engine.wait_ge(sem, count)




def conv_seq(nc, x, rows_w, rows_p, scal, wg_t, w_conv, win_t, wout_t, ident_in, near_in, chain_in,
             flip_in, cas_in, bins_in, region_in, gains_in, out):
    with ExitStack() as ctx:
        def sb(name, shape, dt=F32):
            return ctx.enter_context(nc.sbuf_tensor(name, shape, dt))

        def sem(name):
            return ctx.enter_context(nc.semaphore(name))

        tile = [ctx.enter_context(nc.psum_tensor(f"tile{i}", [P, N], F32)) for i in range(2)]
        acc0 = ctx.enter_context(nc.psum_tensor("acc0", [P, N], F32))
        acc1 = ctx.enter_context(nc.psum_tensor("acc1", [P, N], F32))

        rw = sb("rw", [P, 5, P])
        rp = sb("rp", [P, 5, 6])
        sc = sb("sc", [P, 2])
        wgT = sb("wgT", [P, P])
        wc = sb("wc", [POOL * POOL, P])
        winT = sb("winT", [P, M])
        woutT = sb("woutT", [BM, B, P])
        ident = sb("ident", [P, P])
        near = sb("near", [P, 3, WIN])
        chain = sb("chain", [P, P])
        flip = sb("flip", [P, 2, P])
        cas = sb("cas", [P, CH, N])
        bins = sb("bins", [P, CH, NBINS])
        region = sb("region", [NBINS, 2, CH, P])
        gains = sb("gains", [P, CH, 2])
        identb = sb("identb", [P, P], BF16)
        nearb = sb("nearb", [P, 3, WIN], BF16)
        chainb = sb("chainb", [P, P], BF16)
        std = sb("std", [P, 5])
        var = sb("var", [P, 5])
        rstd = sb("rstd", [P, 5])
        nwt = sb("nwt", [P, 5])
        nwt2 = sb("nwt2", [P, 5])
        nwt3 = sb("nwt3", [P, 5])
        rstd2 = sb("rstd2", [P, 5])
        scale = sb("scale", [P, 5])
        dev = sb("dev", [P, 5])
        dev2 = sb("dev2", [P, 5])
        dev3 = sb("dev3", [P, 5])
        bias = sb("bias", [P, 5])
        vb = sb("vb", [P, 1])
        keep = sb("keep", [P, 1])
        ngama = sb("ngama", [P, 1])
        rws = sb("rws", [P, 5, P])
        wT = sb("wT", [P, 5, P])

        xin = sb("xin", [P, B, N])
        xh = sb("xh", [P, N], F32R)
        xl = sb("xl", [P, N], F32R)
        pooled = sb("pooled", [P, POOL * POOL])
        gapT = sb("gapT", [POOL * POOL, P])
        gate_h = sb("gate_h", [P, P], F32R)
        gate_l = sb("gate_l", [P, P], F32R)
        v0 = sb("v0", [P, CH, P])
        v0n = sb("v0n", [P, CH, P])
        nmax0 = sb("nmax0", [P, CH])
        sum0 = sb("sum0", [P, CH])
        rec0 = sb("rec0", [P, CH])
        e0 = sb("e0", [P, RING, N])
        x1 = sb("x1", [P, N])
        qs = sb("qs", [KS3, N], F32R)
        ks = sb("ks", [KS3, N], F32R)
        qs2 = sb("qs2", [KS3, N], F32R)
        full = sb("full", [KS3, 2, N])
        v1 = sb("v1", [P, CH, P])
        nmax1 = sb("nmax1", [P, CH])
        sum1 = sb("sum1", [P, CH])
        log1 = sb("log1", [P, CH])
        shf = sb("shf", [P, CH])
        shf_h = sb("shf_h", [P, CH], F32R)
        diag = sb("diag", [P, CH, P])
        junk = sb("junk", [P, 2, N], BF16)
        e1 = sb("e1", [P, RING, N])
        x2 = sb("x2", [P, N])
        x2T = sb("x2T", [P, CH, P])
        nmaxc = sb("nmaxc", [P, 1])
        sumc = sb("sumc", [P, 1])
        recc = sb("recc", [P, 1])
        ec = sb("ec", [P, P])
        ecn = sb("ecn", [P, P])
        ecT = sb("ecT", [P, P])
        e2 = sb("e2", [P, CH, WIN])
        xkeep = sb("xkeep", [P, N])
        zneg = sb("zneg", [P, N])
        zexp = sb("zexp", [P, N])
        zelu = sb("zelu", [P, N])
        x3s = sb("x3s", [P, N])
        x3 = xin
        xp = sb("xp", [P, CH, BM])
        hart = sb("hart", [P, CH, BM])
        power = sb("power", [P, CH, BM])
        both = sb("both", [P, CH, BM])
        mag = sb("mag", [P, CH, BM])
        msum = sb("msum", [P, CH, B])
        en = sb("en", [B, NBINS + 2])
        es_a = sb("es_a", [B, NBINS])
        es_b = sb("es_b", [B, NBINS])
        es = sb("es", [B, NBINS + 2])
        pk = [sb(f"pk{i}", [B, NBINS]) for i in range(4)]
        sel = [sb(f"sel{i}", [B, NBINS]) for i in range(6)]
        one = sb("one", [B, 8])
        ramp = sb("ramp", [B, NBINS])
        selT = sb("selT", [NBINS, B])
        enh = sb("enh", [P, 2, CH, B])
        enh2 = sb("enh2", [P, CH, B])
        gain = sb("gain", [P, CH, B])
        coef = sb("coef", [P, CH, BM])
        xe = zneg[0:BM, :]
        yout = x3

        tile_full = [sem(f"tile_full{i}") for i in range(2)]
        names = """x_first_in x_rest_in weights_in const_in cas_in std_ready small_dve bias_ready wfold_ready wT_full wT_ready
            masks_ready diag_zero
            xh_ready xl_ready pooled_ready gapT_ready gate_h_ready gate_ready v0_ready
            nmax0_ready e0_ready rec0_ready v0n_ready e0_used acc0_full x1_ready
            full_ready hi_ready q_ready k_ready v1_ready nmax1_ready sum1_ready log1_ready shf_ready shf_h_ready diag_ready
            qs2_ready e1_ready e1_used acc1_full x2_ready a_ready s_ready
            x2T_ready nmaxc_ready ec_ready recc_ready ecn_ready ecT_ready e2_ready xkeep_ready
            zneg_ready zexp_ready zelu_ready x3s_ready x3_ready xp_ready
            hart_full hart_ready power_ready flip_full both_ready mag_ready msum_ready energy_full
            pick sel_ready selT_full selT_ready enh_full coef_ready enh_chain xe_full xe_ready
            y_full y_ready out_written""".split()
        s = {n: sem(n) for n in names}

        block = ctx.enter_context(nc.Block())

        @block.sync
        def _(sp):
            for b in range(B):
                sp.dma_start(xin[:, b, :], x[b]).then_inc(s["x_rest_in" if b else "x_first_in"], 16)
                if b == 0:
                    for dst, src in ((ident, ident_in), (wgT, wg_t), (wc, w_conv), (rp, rows_p), (rw, rows_w),
                                     (sc, scal)):
                        sp.dma_start(dst[:], src).then_inc(s["weights_in"], 16)
            for dst, src in ((near, near_in), (chain, chain_in), (winT, win_t)):
                sp.dma_start(dst[:], src).then_inc(s["const_in"], 16)
            for dst, src in ((woutT, wout_t), (flip, flip_in), (bins, bins_in), (region, region_in),
                             (gains, gains_in)):
                sp.dma_start(dst[:], src).then_inc(s["cas_in"], 16)
            for j in range(CH):
                sp.dma_start(cas[:, j, :], cas_in[:, j, :]).then_inc(s["cas_in"], 16)
            for b in range(B):
                sp.wait_ge(s["y_ready"], b + 1)
                sp.dma_start(out[b], yout[:, b, :]).then_inc(s["out_written"], 16)
            sp.wait_ge(s["out_written"], 16 * B)

        @block.tensor
        def _(pe):
            def mm(o, lhsT, rhs, start, stop, skip=False):
                return nc.tensor.matmul(o, lhsT, rhs, start=start, stop=stop, skip_group_check=skip)

            pe.wait_ge(s["weights_in"], 16 * 6)
            pe.wait_ge(s["wfold_ready"], 5)
            for k in range(5):
                bank = acc1 if k < 4 else acc0
                last = nc.tensor.transpose(bank[:, (k % 4) * P:(k % 4 + 1) * P], rws[:, k, :], ident[:])
            last.then_inc(s["wT_full"], 1)
            pe.wait_ge(s["wT_ready"], 2)

            for ph in phases(pe):
                a, b = ph.a, ph.b

                def begin(step):
                    last_reader, count = ph.freed(step)
                    if last_reader:
                        pe.wait_ge(s[last_reader], count)
                    return tile[ph.slot(step)]

                def end(step, ins):
                    ins.then_inc(tile_full[ph.slot(step)], 1)

                for step in ph.schedule:
                    name, i = step
                    cols = slice(i * P, (i + 1) * P)
                    if name == "gap":
                        pe.wait_ge(s["pooled_ready"], a + 1)
                        t = begin(step)
                        end(step, mm(t[0:POOL * POOL, 0:P], pooled[:], wgT[:], True, True))
                    elif name == "gate":
                        pe.wait_ge(s["gapT_ready"], a + 1)
                        t = begin(step)
                        end(step, mm(t[:, 0:P], wc[:], gapT[:], True, True))
                    elif name == "val0":
                        pe.wait_ge(s["gate_ready"], a + 1)
                        pe.wait_ge(s["xl_ready"], a + 1)
                        t = begin(step)
                        for u in range(CH):
                            cu = slice(u * P, (u + 1) * P)
                            mm(t[:, cu], xh[:, cu], gate_h[:], True, False)
                            mm(t[:, cu], xh[:, cu], gate_l[:], False, False)
                            last = mm(t[:, cu], xl[:, cu], gate_h[:], False, True)
                        end(step, last)
                    elif name == "gram":
                        pe.wait_ge(s["xl_ready"], a + 1)
                        t = begin(step)
                        for h in range(2):
                            hc = slice(h * HALF, (h + 1) * HALF)
                            mm(t[:, hc], xh[:, cols], xh[:, hc], True, False)
                            mm(t[:, hc], xh[:, cols], xl[:, hc], False, False)
                            last = mm(t[:, hc], xl[:, cols], xh[:, hc], False, True)
                        end(step, last)
                    elif name == "mix":
                        pe.wait_ge(s["e0_ready"], a * CH + i + 1)
                        pe.wait_ge(s["v0n_ready"], a * CH + i + 1)
                        if i == 0:
                            wait_past(pe, s["x1_ready"], a)
                        for h in range(2):
                            hc = slice(h * HALF, (h + 1) * HALF)
                            last = mm(acc0[:, hc], v0n[:, i, :], e0[:, i % RING, hc], i == 0, i == CH - 1)
                        last.then_inc(s["e0_used"], 1)
                    elif name in ("qproj", "kproj", "aproj", "sproj"):
                        k = {"qproj": Q, "kproj": K, "aproj": A_, "sproj": S_}[name]
                        src = x1 if k in (Q, K) else x2
                        pe.wait_ge(s["x1_ready" if k in (Q, K) else "x2_ready"], b + 1)
                        t = begin(step)
                        for h in range(2):
                            hc = slice(h * HALF, (h + 1) * HALF)
                            last = mm(t[0:KS3, hc], wT[:, k, 0:KS3], src[:, hc], True, True)
                        end(step, last)
                    elif name == "val1":
                        pe.wait_ge(s["x1_ready"], b + 1)
                        t = begin(step)
                        for u in range(CH):
                            cu = slice(u * P, (u + 1) * P)
                            last = mm(t[:, cu], x1[:, cu], wT[:, V, :], True, True)
                        end(step, last)
                    elif name == "score":
                        pe.wait_ge(s["q_ready"], b + 1)
                        pe.wait_ge(s["k_ready"], b + 1)
                        t = begin(step)
                        for h in range(2):
                            hc = slice(h * HALF, (h + 1) * HALF)
                            last = mm(t[:, hc], qs[:, cols], ks[:, hc], True, True)
                        end(step, last)
                    elif name in ("shift1", "shift2"):
                        pe.wait_ge(s["diag_ready"], 2 * b + (1 if name == "shift1" else 2))
                        t = begin(step)
                        for u in range(CH):
                            last = nc.tensor.transpose(t[0:KS3, u * P:(u + 1) * P], diag[:, u, 0:KS3], ident[:])
                        end(step, last)
                    elif name == "scoreT":
                        pe.wait_ge(s["qs2_ready"], 2 * b + 1)
                        t = begin(step)
                        for h in range(2):
                            hc = slice(h * HALF, (h + 1) * HALF)
                            last = mm(t[:, hc], ks[:, cols], qs2[:, hc], True, True)
                        end(step, last)
                    elif name == "attend":
                        pe.wait_ge(s["e1_ready"], b * CH + i + 1)
                        pe.wait_ge(s["v1_ready"], b + 1)
                        if i == 0:
                            wait_past(pe, s["zelu_ready"], b)
                        for h in range(2):
                            hc = slice(h * HALF, (h + 1) * HALF)
                            last = mm(acc1[:, hc], v1[:, i, :], e1[:, i % RING, hc], i == 0, i == CH - 1)
                        last.then_inc(s["e1_used"], 1)
                    elif name == "x2T":
                        pe.wait_ge(s["x2_ready"], b + 1)
                        t = begin(step)
                        for u in range(CH):
                            cu = slice(u * P, (u + 1) * P)
                            last = nc.tensor.transpose(t[:, cu], x2[:, cu], ident[:])
                        end(step, last)
                    elif name == "chan":
                        pe.wait_ge(s["x2T_ready"], b + 1)
                        pe.wait_ge(s["masks_ready"], 3)
                        t = begin(step)
                        for u in range(CH):
                            mm(t[:, 0:P], x2T[:, u, :], x2T[:, u, :], u == 0, False)
                        end(step, mm(t[:, 0:P], identb[:], chainb[:], False, True))
                    elif name == "chanT":
                        pe.wait_ge(s["ecn_ready"], b + 1)
                        t = begin(step)
                        end(step, nc.tensor.transpose(t[:, 0:P], ecn[:], ident[:]))
                    elif name in ("near", "nearT"):
                        if name == "near":
                            pe.wait_ge(s["a_ready"], b + 1)
                            pe.wait_ge(s["s_ready"], b + 1)
                            pe.wait_ge(s["masks_ready"], 3)
                            lhs, rhs = qs, ks
                        else:
                            pe.wait_ge(s["qs2_ready"], 2 * b + 2)
                            lhs, rhs = ks, qs2
                        t = begin(step)
                        for u in range(4 * i, 4 * i + 4):
                            kind = 1 if u == 0 else 2 if u == CH - 1 else 0
                            lo, hi = max(u * P - W, 0), min((u + 1) * P + W, N)
                            w0 = (u % 4) * WPAD
                            off = w0 + lo - (u * P - W)
                            first = u % 2 == 0
                            mm(t[:, w0:w0 + WIN], identb[:], nearb[:, kind, :], first, False, True)
                            last = mm(t[:, off:off + hi - lo], lhs[:, u * P:(u + 1) * P], rhs[:, lo:hi],
                                      False, not first, True)
                        end(step, last)
                    elif name == "join":
                        pe.wait_ge(s["ecT_ready"], b + 1)
                        pe.wait_ge(s["e2_ready"], 2 * b + 2)
                        pe.wait_ge(s["x2_ready"], b + 1)
                        for h in range(2):
                            hc = slice(h * HALF, (h + 1) * HALF)
                            mm(acc1[:, hc], ecT[:], x2[:, hc], True, False, True)
                            for u in range(CH):
                                lo = max(u * P - W, h * HALF)
                                hi = min((u + 1) * P + W, (h + 1) * HALF)
                                if lo >= hi:
                                    continue
                                off = lo - (u * P - W)
                                last = mm(acc1[:, lo:hi], x2T[:, u, :], e2[:, u, off:off + hi - lo],
                                          False, u * P + P + W >= (h + 1) * HALF and u in (4, 7), True)
                        last.then_inc(s["acc1_full"], 1)
                    elif name == "xproj":
                        pe.wait_ge(s["x3s_ready"], b + 1)
                        pe.wait_ge(s["const_in"], 16 * 3)
                        t = begin(step)
                        x3v = x3s[:].rearrange("p (r j) -> p j r", j=CH)
                        for u in range(CH):
                            last = mm(t[:, u * M:(u + 1) * M], x3v[:, u], winT[:], True, True)
                        end(step, last)

            pe.wait_ge(s["cas_in"], 16 * (5 + CH))
            pe.wait_ge(s["xp_ready"], B)
            casv = cas[:].rearrange("p u (r j) -> p u j r", j=CH)
            for j in range(CH):
                for u in range(CH):
                    last = mm(acc0[:, j * BM:(j + 1) * BM], casv[:, u, j], xp[:, u, :], u == 0, u == CH - 1)
            last.then_inc(s["hart_full"], 1)
            pe.wait_ge(s["power_ready"], 1)
            for j in range(CH):
                last = mm(acc1[:, j * BM:(j + 1) * BM], flip[:, min(j, 1), :], power[:, (CH - j) % CH, :], True, True)
            last.then_inc(s["flip_full"], 1)
            pe.wait_ge(s["msum_ready"], 1)
            for j in range(CH):
                last = mm(acc0[0:B, HALF:HALF + NBINS], msum[:, j, :], bins[:, j, :], j == 0, j == CH - 1)
            last.then_inc(s["energy_full"], 1)
            pe.wait_ge(s["sel_ready"], 1)
            nc.tensor.transpose(acc1[0:NBINS, HALF:HALF + B], sel[5][:], ident[0:B, 0:B]).then_inc(s["selT_full"], 1)
            pe.wait_ge(s["selT_ready"], 1)
            for side in range(2):
                for j in range(CH):
                    o = (side * CH + j) * B
                    last = mm(acc1[:, HALF + 64 + o:HALF + 64 + o + B], region[:, side, j, :], selT[:], True, True)
            last.then_inc(s["enh_full"], 1)
            pe.wait_ge(s["coef_ready"], 1)
            for h in range(2):
                hc = slice(h * HALF, (h + 1) * HALF)
                for j in range(CH):
                    last = mm(acc0[0:BM, hc], coef[:, j, :], cas[:, j, hc], j == 0, j == CH - 1)
            last.then_inc(s["xe_full"], 1)
            for b in range(B):
                pe.wait_ge(s["xe_ready"], 1)
                t = (acc1, tile[0], tile[1], acc0)[b]
                for h in range(2):
                    hc = slice(h * HALF, (h + 1) * HALF)
                    last = mm(t[:, hc], woutT[:, b, :], xe[:, hc], True, True)
                last.then_inc(s["y_full"], 1)

        @block.scalar
        def _(act):
            act.wait_ge(s["small_dve"], 1)
            nc.scalar.activation(std[:], var[:], ACT.Sqrt).then_inc(s["std_ready"], 1)
            act.wait_ge(s["wT_full"], 1)
            nc.scalar.activation(wT[:, 0:4, :], acc1[:, 0:4 * P].rearrange("p (k c) -> p k c", k=4),
                                 ACT.Copy).then_inc(s["wT_ready"], 1)
            nc.scalar.activation(wT[:, 4, :], acc0[:, 0:P], ACT.Copy).then_inc(s["wT_ready"], 1)

            act.preload_act_table_set("natural_log_exp_and_others")
            for ph in phases(act):
                a, b = ph.a, ph.b

                def take(step):
                    act.wait_ge(tile_full[ph.slot(step)], ph.used(step) + 1)
                    return tile[ph.slot(step)]

                for step in ph.schedule:
                    name, i = step
                    if name == "gap":
                        t = take(step)
                        nc.scalar.activation(gapT[:], t[0:POOL * POOL, 0:P], ACT.Relu,
                                             scale=float(POOL * POOL) / N).then_inc(s["gapT_ready"], 1)
                    elif name == "gate":
                        t = take(step)
                        nc.scalar.activation(gate_h[:], t[:, 0:P], ACT.Copy).then_inc(s["gate_h_ready"], 1)
                    elif name == "val0":
                        t = take(step)
                        wait_past(act, s["v0n_ready"], a * CH)
                        nc.scalar.activation(v0[:].rearrange("p u c -> p (u c)"), t[:, :],
                                             ACT.Copy).then_inc(s["v0_ready"], 1)
                    elif name == "gram":
                        t = take(step)
                        act.wait_ge(s["nmax0_ready"], a * CH + i + 1)
                        wait_past(act, s["e0_used"], a * CH + max(i - RING + 1, 0))
                        nc.scalar.activation(e0[:, i % RING, :], t[:, :], ACT.Exp, bias=nmax0[:, i:i + 1],
                                             accum_out=sum0[:, i:i + 1]).then_inc(s["e0_ready"], 1)
                    elif name in ("qproj", "kproj"):
                        k = Q if name == "qproj" else K
                        t = take(step)
                        act.wait_ge(s["bias_ready"], 2)
                        if k == Q:
                            wait_past(act, s["qs2_ready"], 2 * b)
                        nc.scalar.activation((qs if k == Q else ks)[:], t[0:KS3, :], ACT.Identity,
                                             bias=bias[0:KS3, k:k + 1]).then_inc(s["hi_ready"], 1)
                    elif name in ("aproj", "sproj"):
                        k = A_ if name == "aproj" else S_
                        t = take(step)
                        if k == A_:
                            act.wait_ge(s["e1_ready"], (b + 1) * CH)
                        nc.scalar.activation((qs if k == A_ else ks)[:], t[0:KS3, :], ACT.Relu,
                                             bias=bias[0:KS3, k:k + 1]).then_inc(s["hi_ready"], 1)
                    elif name == "val1":
                        t = take(step)
                        wait_past(act, s["e1_used"], b * CH)
                        nc.scalar.activation(v1[:].rearrange("p u c -> p (u c)"), t[:, :],
                                             ACT.Copy).then_inc(s["v1_ready"], 1)
                    elif name == "score":
                        t = take(step)
                        act.wait_ge(s["nmax1_ready"], b * (CH + 2) + i + 1)
                        wait_past(act, s["sum1_ready"], b * 2 * CH + i - 1)
                        nc.scalar.activation(junk[:, i % 2, :], t[:, :], ACT.Exp, bias=nmax1[:, i:i + 1],
                                             accum_out=sum1[:, i:i + 1]).then_inc(s["sum1_ready"], 1)
                    elif name in ("shift1", "shift2"):
                        r = 1 if name == "shift1" else 2
                        act.wait_ge(s["sum1_ready"], b * 2 * CH + CH * r)
                        nc.scalar.activation(log1[:], sum1[:], ACT.Ln).then_inc(s["log1_ready"], 1)
                    elif name == "scoreT":
                        t = take(step)
                        wait_past(act, s["e1_used"], b * CH + max(i - RING + 1, 0))
                        nc.scalar.activation(e1[:, i % RING, :], t[:, :], ACT.Exp).then_inc(s["e1_ready"], 1)
                    elif name == "x2T":
                        t = take(step)
                        wait_past(act, s["acc1_full"], b)
                        nc.scalar.activation(x2T[:].rearrange("p u c -> p (u c)"), t[:, :],
                                             ACT.Copy).then_inc(s["x2T_ready"], 1)
                    elif name == "xkeep":
                        act.wait_ge(s["x2_ready"], b + 1)
                        wait_past(act, s["x3s_ready"], b)
                        nc.scalar.activation(xkeep[:], x2[:], ACT.Identity, scale=keep[:], bias=ngama[:]
                                             ).then_inc(s["xkeep_ready"], 1)
                    elif name == "chan":
                        t = take(step)
                        act.wait_ge(s["nmaxc_ready"], b + 1)
                        nc.scalar.activation(ec[:], t[:, 0:P], ACT.Exp, bias=nmaxc[:], accum_out=sumc[:]
                                             ).then_inc(s["ec_ready"], 1)
                    elif name == "chanT":
                        t = take(step)
                        nc.scalar.activation(ecT[:], t[:, 0:P], ACT.Copy).then_inc(s["ecT_ready"], 1)
                    elif name == "near":
                        t = take(step)
                        act.wait_ge(s["nmax1_ready"], b * (CH + 2) + CH + i + 1)
                        act.wait_ge(s["sum1_ready"], b * 2 * CH + CH + 4 * i)
                        if i == 0:
                            act.wait_ge(s["shf_ready"], 2 * b + 1)
                        for u in range(4 * i, 4 * i + 4):
                            nc.scalar.activation(junk[:, i, (u % 4) * WPAD:(u % 4) * WPAD + WIN], t[:, (u % 4) * WPAD:(u % 4) * WPAD + WIN], ACT.Exp,
                                                 bias=nmax1[:, u:u + 1], accum_out=sum1[:, u:u + 1]
                                                 ).then_inc(s["sum1_ready"], 1)
                    elif name == "nearT":
                        t = take(step)
                        tv = t[:, :].rearrange("p (u w) -> p u w", w=WPAD)[:, :, 0:WIN]
                        nc.scalar.activation(e2[:, 4 * i:4 * i + 4, :], tv, ACT.Exp).then_inc(s["e2_ready"], 1)
                    elif name == "x3":
                        act.wait_ge(s["zneg_ready"], b + 1)
                        nc.scalar.activation(zexp[:], zneg[:], ACT.Exp).then_inc(s["zexp_ready"], 1)

            act.wait_ge(s["hart_full"], 1)
            nc.scalar.activation(power[:].rearrange("p j m -> p (j m)"), acc0[:, 0:HALF],
                                 ACT.Square).then_inc(s["power_ready"], 1)
            nc.scalar.activation(hart[:].rearrange("p j m -> p (j m)"), acc0[:, 0:HALF],
                                 ACT.Copy).then_inc(s["hart_ready"], 1)
            act.wait_ge(s["both_ready"], 1)
            nc.scalar.activation(mag[:], both[:], ACT.Sqrt, scale=0.5).then_inc(s["mag_ready"], 1)
            act.wait_ge(s["selT_full"], 1)
            nc.scalar.activation(selT[:], acc1[0:NBINS, HALF:HALF + B], ACT.Copy).then_inc(s["selT_ready"], 1)
            act.wait_ge(s["xe_full"], 1)
            nc.scalar.activation(xe[:], acc0[0:BM, :], ACT.Copy).then_inc(s["xe_ready"], 1)

        @block.vector
        def _(dve):
            vec = nc.vector
            par = [rp[:, :, i] for i in range(6)]
            dve.wait_ge(s["weights_in"], 16 * 6)
            vec.tensor_scalar(var[:], par[4], EPS, None, ALU.add).then_inc(s["small_dve"], 1)
            dve.wait_ge(s["std_ready"], 1)
            small = [1]

            def link(ins):
                small[0] += 1
                ins.then_inc(s["small_dve"], 1)
                dve.wait_ge(s["small_dve"], small[0])

            link(vec.reciprocal(rstd[:], std[:]))
            link(vec.tensor_tensor(nwt[:], rstd[:], rstd[:], ALU.mult))
            link(vec.tensor_tensor(nwt2[:], nwt[:], var[:], ALU.mult))
            link(vec.tensor_scalar(nwt3[:], nwt2[:], -0.5, 1.5, ALU.mult, ALU.add))
            link(vec.tensor_tensor(rstd2[:], rstd[:], nwt3[:], ALU.mult))
            link(vec.tensor_tensor(scale[:], rstd2[:], par[1], ALU.mult))
            link(vec.tensor_tensor(dev[:], par[0], par[3], ALU.subtract))
            link(vec.tensor_tensor(dev2[:], dev[:], scale[:], ALU.mult))
            link(vec.tensor_tensor(dev3[:], dev2[:], par[2], ALU.add))
            vec.tensor_tensor(bias[:], dev3[:], par[5], ALU.add).then_inc(s["bias_ready"], 1)
            link(vec.tensor_tensor(scale[:, V:V + 1], scale[:, V:V + 1], sc[:, 0:1], ALU.mult))
            link(vec.tensor_tensor(vb[:], dev3[:, V:V + 1], sc[:, 0:1], ALU.mult))
            link(vec.tensor_scalar(keep[:], sc[:, 1:2], -1.0, 1.0, ALU.mult, ALU.add))
            link(vec.tensor_scalar(ngama[:], sc[:, 1:2], -1.0, None, ALU.mult))
            for k in range(5):
                vec.tensor_scalar(rws[:, k, :], rw[:, k, :], scale[:, k:k + 1], None,
                                  ALU.mult).then_inc(s["wfold_ready"], 1)
            dve.wait_ge(s["bias_ready"], 1)
            dve.sem_inc(s["bias_ready"], 1)

            for ph in phases(dve):
                a, b = ph.a, ph.b

                def take(step):
                    dve.wait_ge(tile_full[ph.slot(step)], ph.used(step) + 1)
                    return tile[ph.slot(step)]

                for step in ph.schedule:
                    name, i = step
                    if name == "split":
                        if isinstance(a, int) and a == 0:
                            dve.wait_ge(s["x_first_in"], 16)
                        else:
                            dve.wait_ge(s["x_rest_in"], 16 * (B - 1))
                            dve.wait_ge(s["e0_used"], a * CH)
                        xa = xin[:, a, :]
                        vec.tensor_copy(xh[:], xa).then_inc(s["xh_ready"], 1)
                        xv = xa.rearrange("p (y r x c) -> p y x r c", y=POOL, r=H // POOL, x=POOL)
                        vec.tensor_reduce(pooled[:].rearrange("p (y x) -> p y x", y=POOL), xv, AX.XY,
                                          ALU.add).then_inc(s["pooled_ready"], 1)
                        dve.wait_ge(s["xh_ready"], a + 1)
                        vec.tensor_tensor(xl[:], xa, xh[:].bitcast(F32), ALU.subtract).then_inc(s["xl_ready"], 1)
                    elif name == "gate":
                        t = take(step)
                        dve.wait_ge(s["gate_h_ready"], a + 1)
                        vec.tensor_tensor(gate_l[:], t[:, 0:P], gate_h[:].bitcast(F32),
                                          ALU.subtract).then_inc(s["gate_ready"], 1)
                    elif name == "gram":
                        t = take(step)
                        vec.tensor_reduce(nmax0[:, i:i + 1], t[:, :], AX.X, ALU.max,
                                          negate=True).then_inc(s["nmax0_ready"], 1)
                    elif name == "norm0":
                        dve.wait_ge(s["e0_ready"], a * CH + i + 1)
                        dve.wait_ge(s["v0_ready"], a + 1)
                        vec.reciprocal(rec0[:, i:i + 1], sum0[:, i:i + 1]).then_inc(s["rec0_ready"], 1)
                        dve.wait_ge(s["rec0_ready"], a * CH + i + 1)
                        vec.tensor_scalar(v0n[:, i, :], v0[:, i, :], rec0[:, i:i + 1], None,
                                          ALU.mult).then_inc(s["v0n_ready"], 1)
                    elif name == "x1":
                        dve.wait_ge(s["e0_used"], (a + 1) * CH)
                        vec.tensor_tensor(x1[:], acc0[:, :], xin[:, a, :], ALU.add).then_inc(s["x1_ready"], 1)
                    elif name in ("qproj", "kproj"):
                        k = Q if name == "qproj" else K
                        r = slice(2 * G, 3 * G) if k == Q else slice(G, 2 * G)
                        dst = (qs if k == Q else ks)[r, :]
                        t = take(step)
                        dve.wait_ge(s["hi_ready"], 4 * b + 1 + (k == K))
                        vec.scalar_tensor_tensor(out=dst, in0=t[r, :], scalar=bias[r, k:k + 1],
                                                 in1=dst.bitcast(F32), op0=ALU.add, op1=ALU.subtract
                                                 ).then_inc(s["q_ready" if k == Q else "k_ready"], 1)
                    elif name in ("aproj", "sproj"):
                        k = A_ if name == "aproj" else S_
                        r = slice(2 * G, 3 * G) if k == A_ else slice(G, 2 * G)
                        dst = (qs if k == A_ else ks)[r, :]
                        t = take(step)
                        dve.wait_ge(s["hi_ready"], 4 * b + 3 + (k == S_))
                        vec.tensor_scalar(full[r, k - A_, :], t[r, :], bias[r, k:k + 1], 0.0, ALU.add,
                                          ALU.max).then_inc(s["full_ready"], 1)
                        dve.wait_ge(s["full_ready"], 2 * b + 1 + (k == S_))
                        vec.tensor_tensor(dst, full[r, k - A_, :], dst.bitcast(F32), ALU.subtract
                                          ).then_inc(s["a_ready" if k == A_ else "s_ready"], 1)
                    elif name == "score":
                        t = take(step)
                        vec.tensor_reduce(nmax1[:, i:i + 1], t[:, :], AX.X, ALU.max,
                                          negate=True).then_inc(s["nmax1_ready"], 1)
                    elif name in ("shift1", "shift2"):
                        n = 2 * b + (1 if name == "shift1" else 2)
                        dve.wait_ge(s["log1_ready"], n)
                        vec.tensor_tensor(shf[:], nmax1[:], log1[:], ALU.subtract).then_inc(s["shf_ready"], 1)
                        dve.wait_ge(s["shf_ready"], n)
                        vec.tensor_copy(shf_h[:], shf[:]).then_inc(s["shf_h_ready"], 1)
                        dve.wait_ge(s["shf_h_ready"], n)
                        dve.wait_ge(s["diag_zero"], 1)
                        flat = diag[:].rearrange("p u c -> p (u c)")
                        d0 = flat[:, HID:HID + (CH - 1) * (P + 1) + 1:P + 1]
                        d2 = flat[:, 2 * G + HID:2 * G + HID + (CH - 1) * (P + 1) + 1:P + 1]
                        vec.tensor_copy(d0, shf_h[:].bitcast(F32))
                        vec.tensor_tensor(d2, shf[:], shf_h[:].bitcast(F32), ALU.subtract
                                          ).then_inc(s["diag_ready"], 1)
                        t = take(step)
                        vec.tensor_tensor(qs2[:], t[0:KS3, :], qs[:].bitcast(F32), ALU.add
                                          ).then_inc(s["qs2_ready"], 1)
                    elif name == "x2":
                        dve.wait_ge(s["e1_used"], (b + 1) * CH)
                        vec.scalar_tensor_tensor(out=x2[:], in0=acc1[:, :], scalar=vb[:], in1=x1[:],
                                                 op0=ALU.add, op1=ALU.add).then_inc(s["x2_ready"], 1)
                    elif name == "near":
                        t = take(step)
                        tv = t[:, :].rearrange("p (u w) -> p u w", w=WPAD)[:, :, 0:WIN]
                        vec.tensor_reduce(nmax1[:, 4 * i:4 * i + 4], tv, AX.X, ALU.max,
                                          negate=True).then_inc(s["nmax1_ready"], 1)
                    elif name == "chan":
                        t = take(step)
                        vec.tensor_reduce(nmaxc[:], t[:, 0:P], AX.X, ALU.max, negate=True
                                          ).then_inc(s["nmaxc_ready"], 1)
                        dve.wait_ge(s["ec_ready"], b + 1)
                        vec.reciprocal(recc[:], sumc[:]).then_inc(s["recc_ready"], 1)
                        dve.wait_ge(s["recc_ready"], b + 1)
                        vec.tensor_scalar(ecn[:], ec[:], recc[:], None, ALU.mult).then_inc(s["ecn_ready"], 1)
                    elif name == "x3":
                        dve.wait_ge(s["acc1_full"], b + 1)
                        vec.tensor_scalar(zneg[:], acc1[:, :], 0.0, None, ALU.min).then_inc(s["zneg_ready"], 1)
                        dve.wait_ge(s["zexp_ready"], b + 1)
                        vec.scalar_tensor_tensor(out=zelu[:], in0=acc1[:, :], scalar=0.0, in1=zexp[:],
                                                 op0=ALU.max, op1=ALU.add).then_inc(s["zelu_ready"], 1)
                        dve.wait_ge(s["zelu_ready"], b + 1)
                        dve.wait_ge(s["xkeep_ready"], b + 1)
                        wait_past(dve, s["x3_ready"], b)
                        vec.scalar_tensor_tensor(out=x3s[:], in0=zelu[:], scalar=sc[:, 1:2], in1=xkeep[:],
                                                 op0=ALU.mult, op1=ALU.add).then_inc(s["x3s_ready"], 1)
                    elif name == "xproj":
                        t = take(step)
                        vec.tensor_copy(xp[:, :, bass.ds(b * M, M)] if not isinstance(b, int)
                                        else xp[:, :, b * M:(b + 1) * M],
                                        t[:, 0:CH * M].rearrange("p (u m) -> p u m", m=M)
                                        ).then_inc(s["xp_ready"], 1)

            dve.wait_ge(s["flip_full"], 1)
            dve.wait_ge(s["power_ready"], 1)
            vec.tensor_tensor(both[:].rearrange("p j m -> p (j m)"), acc1[:, 0:HALF],
                              power[:].rearrange("p j m -> p (j m)"), ALU.add).then_inc(s["both_ready"], 1)
            dve.wait_ge(s["mag_ready"], 1)
            vec.tensor_reduce(msum[:].rearrange("p j b -> p (j b)"), mag[:].rearrange("p j (b m) -> p (j b) m", m=M),
                              AX.X, ALU.add).then_inc(s["msum_ready"], 1)
            count = [0]

            def step(ins):
                count[0] += 1
                ins.then_inc(s["pick"], 1)
                dve.wait_ge(s["pick"], count[0])

            NB = NBINS
            step(vec.memset(en[:], 0.0))
            dve.wait_ge(s["energy_full"], 1)
            step(vec.tensor_scalar(en[:, 1:NB + 1], acc0[0:B, HALF:HALF + NB], 1.0 / M, None, ALU.mult))
            step(vec.tensor_tensor(es_a[:], en[:, 0:NB], en[:, 2:NB + 2], ALU.add))
            step(vec.tensor_scalar(es_b[:], en[:, 1:NB + 1], 0.5, None, ALU.mult))
            step(vec.scalar_tensor_tensor(out=es[:, 1:NB + 1], in0=es_a[:], scalar=0.25, in1=es_b[:],
                                          op0=ALU.mult, op1=ALU.add))
            e = es[:, 1:NB + 1]
            step(vec.tensor_copy(es[:, 0:1], es[:, NB:NB + 1]))
            step(vec.tensor_copy(es[:, NB + 1:NB + 2], es[:, 1:2]))
            step(vec.tensor_reduce(one[:, 0:1], e, AX.X, ALU.add))
            step(vec.tensor_scalar(one[:, 1:2], one[:, 0:1], 1.0 / NB, None, ALU.mult))
            step(vec.tensor_tensor(pk[0][:], e, es[:, 0:NB], ALU.is_gt))
            step(vec.tensor_tensor(pk[1][:], e, es[:, 2:NB + 2], ALU.is_gt))
            step(vec.scalar_tensor_tensor(out=pk[2][:], in0=e, scalar=one[:, 1:2], in1=pk[0][:],
                                          op0=ALU.is_gt, op1=ALU.mult))
            step(vec.tensor_tensor(pk[3][:], pk[2][:], pk[1][:], ALU.mult))
            step(vec.tensor_tensor(pk[0][:], pk[3][:], e, ALU.mult))
            step(vec.tensor_reduce(one[:, 2:3], pk[0][:], AX.X, ALU.max))
            step(vec.tensor_scalar(one[:, 3:4], one[:, 2:3], 0.0, None, ALU.is_equal))
            step(vec.scalar_tensor_tensor(out=pk[1][:], in0=e, scalar=one[:, 3:4], in1=pk[0][:],
                                          op0=ALU.mult, op1=ALU.max))
            dve.wait_ge(s["masks_ready"], 4)

            def first_of_max(vals, top, hit, key, low, pick):
                step(vec.tensor_reduce(top, vals, AX.X, ALU.max))
                step(vec.tensor_scalar(hit, vals, top, None, ALU.is_equal))
                step(vec.tensor_tensor(key, hit, ramp[:], ALU.mult))
                step(vec.tensor_reduce(low, key, AX.X, ALU.min))
                step(vec.tensor_scalar(pick, ramp[:], low, None, ALU.is_equal))

            first_of_max(pk[1][:], one[:, 4:5], sel[0][:], sel[1][:], one[:, 5:6], sel[2][:])
            step(vec.tensor_tensor(sel[0][:], sel[2][:], pk[0][:], ALU.mult))
            step(vec.tensor_tensor(sel[1][:], pk[0][:], sel[0][:], ALU.subtract))
            first_of_max(sel[1][:], one[:, 6:7], pk[2][:], pk[3][:], one[:, 7:8], sel[3][:])
            step(vec.tensor_scalar(one[:, 5:6], one[:, 6:7], 0.0, None, ALU.is_gt))
            vec.scalar_tensor_tensor(out=sel[5][:], in0=sel[3][:], scalar=one[:, 5:6], in1=sel[2][:],
                                     op0=ALU.mult, op1=ALU.add).then_inc(s["sel_ready"], 1)
            dve.wait_ge(s["enh_full"], 1)
            vec.tensor_scalar(enh[:].rearrange("p s j b -> p (s j b)"), acc1[:, HALF + 64:HALF + 64 + 2 * CH * B],
                              1.0, None, ALU.min).then_inc(s["enh_chain"], 1)
            dve.wait_ge(s["enh_chain"], 1)
            vec.tensor_tensor(enh2[:], enh[:, 0], enh[:, 1], ALU.add).then_inc(s["enh_chain"], 1)
            dve.wait_ge(s["enh_chain"], 2)
            vec.tensor_tensor(gain[:], enh2[:], gains[:, :, 1:2].to_broadcast([P, CH, B]), ALU.mult
                              ).then_inc(s["enh_chain"], 1)
            dve.wait_ge(s["enh_chain"], 3)
            vec.tensor_tensor(enh2[:], gain[:], gains[:, :, 0:1].to_broadcast([P, CH, B]), ALU.add
                              ).then_inc(s["enh_chain"], 1)
            dve.wait_ge(s["enh_chain"], 4)
            dve.wait_ge(s["hart_ready"], 1)
            e2v = enh2[:].rearrange("p j b -> p (j b)").unsqueeze(2).to_broadcast([P, CH * B, M])
            vec.tensor_tensor(coef[:].rearrange("p j (b m) -> p (j b) m", m=M),
                              hart[:].rearrange("p j (b m) -> p (j b) m", m=M), e2v, ALU.mult
                              ).then_inc(s["coef_ready"], 1)
            for b in range(B):
                t = (acc1, tile[0], tile[1], acc0)[b]
                dve.wait_ge(s["y_full"], b + 1)
                dve.wait_ge(s["x3_ready"], B)
                vec.tensor_tensor(yout[:, b, :], t[:, :], x3[:, b, :], ALU.add).then_inc(s["y_ready"], 1)

        @block.gpsimd
        def _(pool):
            gp = nc.gpsimd
            gp.memset(diag[:], 0.0).then_inc(s["diag_zero"], 1)
            pool.wait_ge(s["weights_in"], 16 * 6)
            pool.wait_ge(s["const_in"], 16 * 3)
            gp.tensor_copy(identb[:], ident[:]).then_inc(s["masks_ready"], 1)
            gp.tensor_copy(nearb[:], near[:]).then_inc(s["masks_ready"], 1)
            gp.tensor_copy(chainb[:], chain[:]).then_inc(s["masks_ready"], 1)
            gp.iota(ramp[:], pattern=[[1, NBINS]], base=-NBINS, channel_multiplier=0,
                    allow_small_or_imprecise_dtypes=True).then_inc(s["masks_ready"], 1)
            for ph in phases(pool):
                b = ph.b
                for step in ph.schedule:
                    name, i = step
                    if name == "x3":
                        pool.wait_ge(s["x3s_ready"], b + 1)
                        gp.tensor_copy(x3[:, b, :], x3s[:]).then_inc(s["x3_ready"], 1)


def _tables():
    f = np.float32
    idx = np.arange(N)
    kh, kw = idx // W, idx % W
    turn = (np.outer(kh, kh) + np.outer(kw, kw)) % H
    ang = 2 * np.pi * np.arange(H) / H
    cas = ((np.cos(ang) + np.sin(ang)) / H)[turn].astype(f)
    order = idx.reshape(P, CH).T
    cas = np.ascontiguousarray(cas[order].transpose(1, 0, 2))
    neg = ((-kh) % H) * W + (-kw) % W
    where = np.empty(N, int)
    where[order.ravel()] = np.arange(N) % P
    flip = np.zeros((P, 2, P), f)
    for kind, j in ((0, 0), (1, 1)):
        for p in range(P):
            flip[where[neg[order[j, p]]], kind, p] = 1
    pi = f(np.pi)
    y, xx = ((kh + H // 2) % H).astype(f), ((kw + W // 2) % W).astype(f)
    r = np.sqrt((y - H // 2) ** 2 + (xx - W // 2) ** 2)
    theta = (np.arctan2((y - f(H // 2)).astype(float), xx - f(W // 2)).astype(f) + pi).astype(f)
    high = (r > f(0.3 * (H // 2))).astype(f)
    edges = _edges()
    mod = np.mod(theta, pi).astype(f)
    bin_of = np.clip(np.searchsorted(edges, mod, side="left") - 1, 0, NBINS - 1)
    onehot = np.zeros((N, NBINS), f)
    onehot[idx, bin_of] = high
    bins = np.ascontiguousarray(onehot[order].transpose(1, 0, 2))
    centre = ((edges[:-1] + edges[1:]) * f(0.5)).astype(f)
    diff = np.abs(theta[None] - centre[:, None])
    diff = np.minimum(diff, pi - diff)
    inside = ((diff <= f(np.radians(15.0))) & (high[None] > 0)).astype(f)
    region = np.stack([inside[:, order], inside[:, neg[order]]], 1)
    assert (high == high[neg]).all()
    gains = np.stack([np.where(high > 0, f(0.8), f(1.0)), f(0.2) * high], -1).astype(f)[order].transpose(1, 0, 2)
    n, m = np.arange(P), np.arange(WIN)
    di = np.abs((n // W + 1)[:, None] - (m // W)[None])
    dj = np.abs((n % W)[:, None] - (m % W)[None])
    adj = (di <= 1) & (dj <= 1) & ~((di == 0) & (dj == 0))
    near = np.full((P, 3, WIN), -9e15, f)
    for kind, ok in enumerate((m >= 0, m >= W, m < WIN - W)):
        near[:, kind][adj & ok[None]] = 0
    c = np.arange(C)
    chain = np.where(np.abs(c[:, None] - c[None]) == 1, f(0), f(-9e15)).astype(f)
    return dict(ident_in=np.eye(P, dtype=f), near_in=near, chain_in=chain, flip_in=flip, cas_in=cas, bins_in=bins,
                region_in=np.ascontiguousarray(region), gains_in=np.ascontiguousarray(gains))


def _edges():
    f = np.float32
    inner = np.arange(NBINS, dtype=f) * (f(1) / f(NBINS) * f(np.pi))
    return np.concatenate([inner, np.array([np.pi], f)])


def _pack(i):
    f = np.float32
    rows_w, rows_p = np.zeros((P, 5, P), f), np.zeros((P, 5, 6), f)
    keys = {Q: "L1_conv_q_", K: "L1_conv_k_", V: "L1_conv_v_"}
    for k, pre in keys.items():
        for g in ([0] if k == V else range(3)):
            at = slice(0, P) if k == V else slice(g * G, g * G + HID)
            rows_w[at, k] = i[pre + "w"]
            for n, part in enumerate(("b", "g", "beta", "mean", "var")):
                rows_p[at, k, n] = i[pre + part]
    for k, t in ((A_, "a"), (S_, "s")):
        for g in range(3):
            at = slice(g * G, g * G + HID)
            rows_w[at, k] = i[f"L2_conv_w{t}"]
            for n, part in ((1, "g"), (2, "b"), (3, "m"), (4, "v")):
                rows_p[at, k, n] = i[f"L2_conv_{part}{t}"]
    for g in range(3):
        for k in (K, S_):
            rows_p[g * G + HID:g * G + HID + CH, k, 5] = 1
    return rows_w, rows_p


def kernel(**inputs):
    import numpy as _np
    import concourse.bacc as _bacc
    from concourse import mybir as _mybir
    from concourse.bass_utils import run_bass_kernel_spmd as _run

    i = {k: _np.asarray(v) for k, v in inputs.items()}
    rows_w, rows_p = _pack(i)
    wout = _np.zeros((BM, B, P), _np.float32)
    for b in range(B):
        wout[b * M:(b + 1) * M, b] = i["L3_conv_w_out"].T
    scal = _np.zeros((P, 2), _np.float32)
    scal[:, 0] = i["L1_conv_gamma"][0]
    scal[:, 1] = i["L2_conv_gama"][0]
    data = dict(x=i["x"].reshape(B, C, N), rows_w=rows_w, rows_p=rows_p, scal=scal, wg_t=i["L0_conv_w_gap"].T,
                w_conv=i["L0_conv_w_conv"], win_t=i["L3_conv_w_in"].T, wout_t=wout, **_tables())
    nc = _bacc.Bacc("TRN2", target_bir_lowering=False, num_devices=1)
    arrays, args = {}, {}
    for name, v in data.items():
        v = _np.ascontiguousarray(v)
        arrays["in_" + name] = v
        args[name] = nc.dram_tensor("in_" + name, v.shape, _mybir.dt.from_np(v.dtype), kind="ExternalInput").ap()
    args["out"] = nc.dram_tensor("out_0", (B, C, N), _mybir.dt.float32, kind="ExternalOutput").ap()
    conv_seq(nc, **args)
    r = _run(nc, [arrays], core_ids=[0])
    return r.results[0]["out_0"].reshape(B, C, H, W)
```

```python
from contextlib import ExitStack

import numpy as np
import concourse.bass as bass
from concourse import mybir

ALU = mybir.AluOpType
ACT = mybir.ActivationFunctionType
AX = mybir.AxisListType
F32 = mybir.dt.float32
F32R = mybir.dt.float32r
BF16 = mybir.dt.bfloat16

P = 128
B, C, H, W = 4, 128, 32, 32
N = H * W
HALF = N // 2
CH = N // P
POOL = 8
HID = C // 8
G = 32
KS3 = 3 * G
WIN = P + 2 * W
WPAD = 256
M = 16
BM = B * M
NBINS = 90
EPS = 1e-5
Q, K, A_, S_, V = range(5)
RING = 3

def l0_chunk(i):
    s = [("gram", i)] if i < CH else []
    s += [("norm0", i - 1)] if 1 <= i <= CH else []
    return s + ([("mix", i - 2)] if i >= 2 else [])


L0 = [l0_chunk(i) for i in range(CH + 2)]
L0_ALL = ([("split", 0), ("gap", 0), ("gate", 0), ("val0", 0)] + sum(L0[:4], []) + [("fold", 0)] + sum(L0[4:], [])
          + [("x1", 0)])


def l12(gap, gate, val0, fill):
    s = [("qproj", 0)] + gap + [("kproj", 0)] + gate + [("val1", 0)] + val0
    for i in range(CH):
        s += fill["score", i] + [("score", i)]
    s += [("shift1", 0)]
    for j in range(CH):
        s += [("scoreT", j)] + ([("attend", j - 1)] if j else []) + fill["attend", j]
    s += [("attend", CH - 1)] + fill["x2", 0] + [("x2", 0), ("aproj", 0), ("sproj", 0), ("x2T", 0)] + fill["x2T", 0]
    s += [("chan", 0), ("near", 0), ("near", 1), ("xkeep", 0), ("chanT", 0)] + fill["near", 0] + [("shift2", 0)]
    s += fill["shift2", 0] + [("nearT", 0), ("nearT", 1)] + fill["nearT", 0] + [("join", 0)]
    return s + fill["join", 0] + [("x3", 0)] + fill["x3", 0] + [("xproj", 0)]


class Fill(dict):

    def __missing__(self, key):
        return []


STEADY = [("split", 0)] + l12([("gap", 0)], [("gate", 0)], [("val0", 0)], Fill({
    ("score", 1): L0[0], ("score", 3): L0[1], ("score", 5): L0[2], ("score", 7): L0[3],
    ("attend", 0): [], ("x2", 0): L0[4], ("x2T", 0): [], ("near", 0): L0[5], ("nearT", 0): L0[6],
    ("join", 0): L0[7], ("x3", 0): L0[8] + L0[9] + [("x1", 0)]}))
L12_ALL = l12([], [], [], Fill())

ACC1 = 2
LAST_READER = {"fold": ("wT_ready", "a", 1, lambda i: 1),
               "gap": ("gapT_ready", "a", 1, lambda i: 1), "gate": ("gate_ready", "a", 1, lambda i: 1),
               "val0": ("v0_ready", "a", 1, lambda i: 1), "gram": ("e0_ready", "a", CH, lambda i: i + 1),
               "qproj": ("q_ready", "b", 1, lambda i: 1), "kproj": ("k_ready", "b", 1, lambda i: 1),
               "val1": ("v1_ready", "b", 1, lambda i: 1), "score": ("sum1_ready", "b", 2 * CH, lambda i: i + 1),
               "shift1": ("qs2_ready", "b", 2, lambda i: 1), "shift2": ("qs2_ready", "b", 2, lambda i: 2),
               "scoreT": ("e1_ready", "b", CH, lambda i: i + 1), "aproj": ("full_ready", "b", 2, lambda i: 1),
               "sproj": ("full_ready", "b", 2, lambda i: 2), "x2T": ("x2T_ready", "b", 1, lambda i: 1),
               "chan": ("ec_ready", "b", 1, lambda i: 1), "chanT": ("ecT_ready", "b", 1, lambda i: 1),
               "near": ("sum1_ready", "b", 2 * CH, lambda i: CH + 4 * i + 4),
               "nearT": ("e2_ready", "b", 2, lambda i: i + 1), "xproj": ("xp_ready", "b", 1, lambda i: 1),
               "attend": ("x2_ready", "b", 1, lambda i: 1), "join": ("zelu_ready", "b", 1, lambda i: 1)}


class Plan:

    def __init__(self, schedule):
        self.schedule, self.slot, self.nth, self.prior = schedule, {}, {}, {}
        self.fills, self.last = [0, 0, 0], [None, None, None]
        age, held = [0, 1, 2], False
        for at, step in enumerate(schedule):
            name, i = step
            if step in (("x2", 0), ("x3", 0)):
                held = False
            accumulates = name == "join" or step == ("attend", 0)
            if name not in LAST_READER or (name == "attend" and i):
                continue
            if accumulates:
                slot, held = ACC1, True
            else:
                slot = min((0, 1) if held else (0, 1, ACC1), key=lambda k: age[k])
            self.slot[step], self.prior[step] = slot, self.last[slot]
            age[slot], self.last[slot] = at + 3, step
            if not accumulates:
                self.nth[step] = self.fills[slot]
                self.fills[slot] += 1


FIRST_PLAN, STEADY_PLAN, LAST_PLAN = Plan(L0_ALL), Plan(STEADY), Plan(L12_ALL)


class Phase:

    def __init__(self, plan, a, b, turns=0, before=None):
        self.plan, self.schedule, self.a, self.b, self.turns, self.before = plan, plan.schedule, a, b, turns, before

    def slot(self, step):
        return self.plan.slot[step]

    def filled(self, step):
        k = self.plan.slot[step]
        base = 0 if self.before is None else FIRST_PLAN.fills[k]
        return base + self.turns * STEADY_PLAN.fills[k] + self.plan.nth[step] + 1

    def freed(self, step):
        a, b, prior = self.a, self.b, self.plan.prior[step]
        if prior is None:
            if self.before is None:
                return None, 0
            prior = self.before.last[self.plan.slot[step]]
            a = self.b if self.a is None else self.a - 1
            b = None if self.b is None else self.b - 1
            if prior is None:
                return None, 0
        name, i = prior
        sem, which, per_image, at = LAST_READER[name]
        return sem, (a if which == "a" else b) * per_image + at(i)


def phases(engine):
    yield Phase(FIRST_PLAN, 0, None)
    yield Phase(STEADY_PLAN, 1, 0, 0, FIRST_PLAN)
    with engine.Fori(1, B - 1) as t:
        yield Phase(STEADY_PLAN, t + 1, t, t, STEADY_PLAN)
    yield Phase(LAST_PLAN, None, B - 1, B - 1, STEADY_PLAN)


def wait_past(engine, sem, count):
    if not (isinstance(count, int) and count <= 0):
        engine.wait_ge(sem, count)




def conv_seq(nc, x, rows_w, rows_p, scal, wg_t, w_conv, win_t, wout_t, ident_in, near_in, chain_in,
             flip_in, cas_in, bins_in, region_in, gains_in, out):
    with ExitStack() as ctx:
        def sb(name, shape, dt=F32):
            return ctx.enter_context(nc.sbuf_tensor(name, shape, dt))

        def sem(name):
            return ctx.enter_context(nc.semaphore(name))

        tile = [ctx.enter_context(nc.psum_tensor(f"tile{i}", [P, N], F32)) for i in range(2)]
        acc0 = ctx.enter_context(nc.psum_tensor("acc0", [P, N], F32))
        acc1 = ctx.enter_context(nc.psum_tensor("acc1", [P, N], F32))
        slots = (tile[0], tile[1], acc1)

        rw = sb("rw", [P, 5, P])
        rp = sb("rp", [P, 5, 6])
        sc = sb("sc", [P, 2])
        wgT = sb("wgT", [P, P])
        wc = sb("wc", [POOL * POOL, P])
        winT = sb("winT", [P, M])
        woutT = sb("woutT", [BM, B, P])
        ident = sb("ident", [P, P])
        near = sb("near", [P, 3, WIN])
        chain = sb("chain", [P, P])
        flip = sb("flip", [P, 2, P])
        cas = sb("cas", [P, CH, N])
        bins = sb("bins", [P, CH, NBINS])
        gains = sb("gains", [P, CH, 2])
        identb = sb("identb", [P, P], BF16)
        nearb = sb("nearb", [P, 3, WIN], BF16)
        chainb = sb("chainb", [P, P], BF16)
        std = sb("std", [P, 5])
        var = sb("var", [P, 5])
        rstd = sb("rstd", [P, 5])
        nwt = sb("nwt", [P, 5])
        nwt2 = sb("nwt2", [P, 5])
        nwt3 = sb("nwt3", [P, 5])
        rstd2 = sb("rstd2", [P, 5])
        scale = sb("scale", [P, 5])
        dev = sb("dev", [P, 5])
        dev2 = sb("dev2", [P, 5])
        dev3 = sb("dev3", [P, 5])
        bias = sb("bias", [P, 5])
        vb = sb("vb", [P, 1])
        keep = sb("keep", [P, 1])
        ngama = sb("ngama", [P, 1])
        rws = sb("rws", [P, 5, P])
        wT = sb("wT", [P, 5, P])

        xin = sb("xin", [P, B, N])
        xh = sb("xh", [P, N], F32R)
        xl = sb("xl", [P, N], F32R)
        pooled = sb("pooled", [P, POOL * POOL])
        gapT = sb("gapT", [POOL * POOL, P])
        gate_h = sb("gate_h", [P, P], F32R)
        gate_l = sb("gate_l", [P, P], F32R)
        v0 = sb("v0", [P, CH, P])
        v0n = sb("v0n", [P, CH, P])
        nmax0 = sb("nmax0", [P, CH])
        sum0 = sb("sum0", [P, CH])
        rec0 = sb("rec0", [P, CH])
        e0 = sb("e0", [P, RING, N])
        x1 = sb("x1", [P, N])
        qs = sb("qs", [KS3, N], F32R)
        ks = sb("ks", [KS3, N], F32R)
        qs2 = sb("qs2", [KS3, N], F32R)
        full = sb("full", [KS3, 2, N])
        v1 = sb("v1", [P, CH, P])
        nmax1 = sb("nmax1", [P, CH])
        sum1 = sb("sum1", [P, CH])
        log1 = sb("log1", [P, CH])
        shf = sb("shf", [P, CH])
        shf_h = sb("shf_h", [P, CH], F32R)
        diag = sb("diag", [P, CH, P])
        junk = sb("junk", [P, 2, N], BF16)
        e1 = sb("e1", [P, RING, N])
        x2 = sb("x2", [P, N])
        x2T = sb("x2T", [P, CH, P])
        nmaxc = sb("nmaxc", [P, 1])
        sumc = sb("sumc", [P, 1])
        recc = sb("recc", [P, 1])
        ec = sb("ec", [P, P])
        ecn = sb("ecn", [P, P])
        ecT = sb("ecT", [P, P])
        e2 = sb("e2", [P, CH, WIN])
        xkeep = sb("xkeep", [P, N])
        zneg = sb("zneg", [P, N])
        zexp = sb("zexp", [P, N])
        zelu = sb("zelu", [P, N])
        x3s = sb("x3s", [P, N])
        x3 = xin
        xp = sb("xp", [P, CH, BM])
        hart = sb("hart", [P, CH, BM])
        power = sb("power", [P, CH, BM])
        both = sb("both", [P, CH, BM])
        mag = sb("mag", [P, CH, BM])
        msum = sb("msum", [P, CH, B])
        en = sb("en", [B, NBINS + 2])
        es_a = sb("es_a", [B, NBINS])
        es = sb("es", [B, NBINS + 2])
        pk = [sb(f"pk{i}", [B, NBINS]) for i in range(4)]
        sel = [sb(f"sel{i}", [B, NBINS]) for i in range(6)]
        one = sb("one", [B, 8])
        ramp = sb("ramp", [B, NBINS])
        selT = sb("selT", [NBINS, B], BF16)
        freq = zneg[0:BM, :]
        regionb = sb("regionb", [NBINS, 2, CH, P], BF16)
        enh = sb("enh", [P, 2, CH, B])
        enh2 = sb("enh2", [P, CH, B])
        gain = sb("gain", [P, CH, B])
        coef = sb("coef", [P, CH, BM])
        xe = zexp[0:BM, :]
        yout = x3

        region = zelu[0:NBINS, :].rearrange("p (j c) -> p j c", c=P)
        tile_full = [sem(f"tile_full{i}") for i in range(3)]
        names = """x_first_in x_rest_in weights_in const_in cas_in std_ready small_dve bias_ready wfold_ready wT_full wT_ready
            masks_ready diag_zero
            xh_ready xl_ready pooled_ready gapT_ready gate_h_ready gate_ready v0_ready
            nmax0_ready e0_ready rec0_ready v0n_ready e0_used acc0_full x1_ready
            full_ready hi_ready q_ready k_ready v1_ready nmax1_ready sum1_ready log1_ready shf_ready shf_h_ready diag_ready
            qs2_ready e1_ready e1_used acc1_full x2_ready a_ready s_ready
            x2T_ready nmaxc_ready ec_ready recc_ready ecn_ready ecT_ready e2_ready xkeep_ready
            zneg_ready zexp_ready zelu_ready x3s_ready x3_ready xp_ready
            freq_full freq_ready region_in hart_full hart_ready power_ready flip_full both_ready mag_ready msum_ready energy_full
            pick sel_ready selT_full selT_ready enh_full coef_ready enh_chain xe_full xe_ready
            y_full y_ready out_written""".split()
        s = {n: sem(n) for n in names}

        block = ctx.enter_context(nc.Block())

        @block.sync
        def _(sp):
            for b in range(B):
                sp.dma_start(xin[:, b, :], x[b]).then_inc(s["x_rest_in" if b else "x_first_in"], 16)
                if b == 0:
                    for dst, src in ((ident, ident_in), (wgT, wg_t), (wc, w_conv), (rp, rows_p), (rw, rows_w),
                                     (sc, scal)):
                        sp.dma_start(dst[:], src).then_inc(s["weights_in"], 16)
            for dst, src in ((near, near_in), (chain, chain_in), (winT, win_t)):
                sp.dma_start(dst[:], src).then_inc(s["const_in"], 16)
            for dst, src in ((woutT, wout_t), (flip, flip_in), (bins, bins_in), (gains, gains_in)):
                sp.dma_start(dst[:], src).then_inc(s["cas_in"], 16)
            for side in range(2):
                if side:
                    sp.wait_ge(s["masks_ready"], 4)
                sp.dma_start(region, region_in[:, side]).then_inc(s["region_in"], 16)
            for j in range(CH):
                sp.dma_start(cas[:, j, :], cas_in[:, j, :]).then_inc(s["cas_in"], 16)
            for b in range(B):
                sp.wait_ge(s["y_ready"], b + 1)
                sp.dma_start(out[b], yout[:, b, :]).then_inc(s["out_written"], 16)
            sp.wait_ge(s["out_written"], 16 * B)

        @block.tensor
        def _(pe):
            def mm(o, lhsT, rhs, start, stop, skip=False):
                return nc.tensor.matmul(o, lhsT, rhs, start=start, stop=stop, skip_group_check=skip)


            for ph in phases(pe):
                a, b = ph.a, ph.b

                def begin(step, waited=None):
                    last_reader, count = ph.freed(step)
                    if last_reader and last_reader != waited:
                        pe.wait_ge(s[last_reader], count)
                    return slots[ph.slot(step)]

                def end(step, ins):
                    ins.then_inc(tile_full[ph.slot(step)], 1)

                for step in ph.schedule:
                    name, i = step
                    cols = slice(i * P, (i + 1) * P)
                    if name == "fold":
                        pe.wait_ge(s["wfold_ready"], 5)
                        t = begin(step)
                        for k in range(5):
                            last = nc.tensor.transpose(t[:, k * P:(k + 1) * P], rws[:, k, :], ident[:])
                        end(step, last)
                    elif name == "gap":
                        pe.wait_ge(s["pooled_ready"], a + 1)
                        if isinstance(a, int) and a == 0:
                            pe.wait_ge(s["weights_in"], 16 * 6)
                        t = begin(step)
                        end(step, mm(t[0:POOL * POOL, 0:P], pooled[:], wgT[:], True, True))
                    elif name == "gate":
                        pe.wait_ge(s["gapT_ready"], a + 1)
                        t = begin(step)
                        end(step, mm(t[:, 0:P], wc[:], gapT[:], True, True))
                    elif name == "val0":
                        pe.wait_ge(s["gate_ready"], a + 1)
                        pe.wait_ge(s["xl_ready"], a + 1)
                        t = begin(step)
                        for u in range(CH):
                            cu = slice(u * P, (u + 1) * P)
                            mm(t[:, cu], xh[:, cu], gate_h[:], True, False)
                            mm(t[:, cu], xh[:, cu], gate_l[:], False, False)
                            last = mm(t[:, cu], xl[:, cu], gate_h[:], False, True)
                        end(step, last)
                    elif name == "gram":
                        pe.wait_ge(s["xl_ready"], a + 1)
                        t = begin(step)
                        for h in range(2):
                            hc = slice(h * HALF, (h + 1) * HALF)
                            mm(t[:, hc], xh[:, cols], xh[:, hc], True, False)
                            mm(t[:, hc], xh[:, cols], xl[:, hc], False, False)
                            last = mm(t[:, hc], xl[:, cols], xh[:, hc], False, True)
                        end(step, last)
                    elif name == "mix":
                        pe.wait_ge(s["e0_ready"], a * CH + i + 1)
                        pe.wait_ge(s["v0n_ready"], a * CH + i + 1)
                        if i == 0:
                            wait_past(pe, s["x1_ready"], a)
                        for h in range(2):
                            hc = slice(h * HALF, (h + 1) * HALF)
                            last = mm(acc0[:, hc], v0n[:, i, :], e0[:, i % RING, hc], i == 0, i == CH - 1)
                        last.then_inc(s["e0_used"], 1)
                    elif name in ("qproj", "kproj", "aproj", "sproj"):
                        k = {"qproj": Q, "kproj": K, "aproj": A_, "sproj": S_}[name]
                        src = x1 if k in (Q, K) else x2
                        pe.wait_ge(s["x1_ready" if k in (Q, K) else "x2_ready"], b + 1)
                        if k == Q:
                            pe.wait_ge(s["wT_ready"], 1)
                        t = begin(step)
                        for h in range(2):
                            hc = slice(h * HALF, (h + 1) * HALF)
                            last = mm(t[0:KS3, hc], wT[:, k, 0:KS3], src[:, hc], True, True)
                        end(step, last)
                    elif name == "val1":
                        pe.wait_ge(s["x1_ready"], b + 1)
                        t = begin(step)
                        for u in range(CH):
                            cu = slice(u * P, (u + 1) * P)
                            last = mm(t[:, cu], x1[:, cu], wT[:, V, :], True, True)
                        end(step, last)
                    elif name == "score":
                        pe.wait_ge(s["q_ready"], b + 1)
                        pe.wait_ge(s["k_ready"], b + 1)
                        t = begin(step)
                        for h in range(2):
                            hc = slice(h * HALF, (h + 1) * HALF)
                            last = mm(t[:, hc], qs[:, cols], ks[:, hc], True, True)
                        end(step, last)
                    elif name in ("shift1", "shift2"):
                        pe.wait_ge(s["diag_ready"], 2 * b + (1 if name == "shift1" else 2))
                        t = begin(step)
                        for u in range(CH):
                            last = nc.tensor.transpose(t[0:KS3, u * P:(u + 1) * P], diag[:, u, 0:KS3], ident[:])
                        end(step, last)
                    elif name == "scoreT":
                        pe.wait_ge(s["qs2_ready"], 2 * b + 1)
                        t = begin(step, "qs2_ready")
                        for h in range(2):
                            hc = slice(h * HALF, (h + 1) * HALF)
                            last = mm(t[:, hc], ks[:, cols], qs2[:, hc], True, True)
                        end(step, last)
                    elif name == "attend":
                        pe.wait_ge(s["e1_ready"], b * CH + i + 1)
                        pe.wait_ge(s["v1_ready"], b + 1)
                        if i == 0:
                            begin(step)
                        for h in range(2):
                            hc = slice(h * HALF, (h + 1) * HALF)
                            last = mm(acc1[:, hc], v1[:, i, :], e1[:, i % RING, hc], i == 0, i == CH - 1)
                        last.then_inc(s["e1_used"], 1)
                    elif name == "x2T":
                        pe.wait_ge(s["x2_ready"], b + 1)
                        t = begin(step)
                        for u in range(CH):
                            cu = slice(u * P, (u + 1) * P)
                            last = nc.tensor.transpose(t[:, cu], x2[:, cu], ident[:])
                        end(step, last)
                    elif name == "chan":
                        pe.wait_ge(s["x2T_ready"], b + 1)
                        pe.wait_ge(s["masks_ready"], 3)
                        t = begin(step)
                        for u in range(CH):
                            mm(t[:, 0:P], x2T[:, u, :], x2T[:, u, :], u == 0, False)
                        end(step, mm(t[:, 0:P], identb[:], chainb[:], False, True))
                    elif name == "chanT":
                        pe.wait_ge(s["ecn_ready"], b + 1)
                        t = begin(step)
                        end(step, nc.tensor.transpose(t[:, 0:P], ecn[:], ident[:]))
                    elif name in ("near", "nearT"):
                        if name == "near":
                            pe.wait_ge(s["a_ready"], b + 1)
                            pe.wait_ge(s["s_ready"], b + 1)
                            pe.wait_ge(s["masks_ready"], 3)
                            lhs, rhs = qs, ks
                        else:
                            pe.wait_ge(s["qs2_ready"], 2 * b + 2)
                            lhs, rhs = ks, qs2
                        t = begin(step, "qs2_ready")
                        for u in range(4 * i, 4 * i + 4):
                            kind = 1 if u == 0 else 2 if u == CH - 1 else 0
                            lo, hi = max(u * P - W, 0), min((u + 1) * P + W, N)
                            w0 = (u % 4) * WPAD
                            off = w0 + lo - (u * P - W)
                            first = u % 2 == 0
                            mm(t[:, w0:w0 + WIN], identb[:], nearb[:, kind, :], first, False, True)
                            last = mm(t[:, off:off + hi - lo], lhs[:, u * P:(u + 1) * P], rhs[:, lo:hi],
                                      False, not first, True)
                        end(step, last)
                    elif name == "join":
                        pe.wait_ge(s["ecT_ready"], b + 1)
                        pe.wait_ge(s["e2_ready"], 2 * b + 2)
                        begin(step, "e2_ready")
                        for h in range(2):
                            hc = slice(h * HALF, (h + 1) * HALF)
                            mm(acc1[:, hc], ecT[:], x2[:, hc], True, False, True)
                            for u in range(CH):
                                lo = max(u * P - W, h * HALF)
                                hi = min((u + 1) * P + W, (h + 1) * HALF)
                                if lo >= hi:
                                    continue
                                off = lo - (u * P - W)
                                last = mm(acc1[:, lo:hi], x2T[:, u, :], e2[:, u, off:off + hi - lo],
                                          False, u * P + P + W >= (h + 1) * HALF and u in (4, 7), True)
                        last.then_inc(s["acc1_full"], 1)
                    elif name == "xproj":
                        pe.wait_ge(s["x3s_ready"], b + 1)
                        pe.wait_ge(s["const_in"], 16 * 3)
                        t = begin(step)
                        x3v = x3s[:].rearrange("p (r j) -> p j r", j=CH)
                        for u in range(CH):
                            last = mm(t[:, u * M:(u + 1) * M], x3v[:, u], winT[:], True, True)
                        end(step, last)

            pe.wait_ge(s["cas_in"], 16 * (4 + CH))
            pe.wait_ge(s["xp_ready"], B)
            for h in range(2):
                hc = slice(h * HALF, (h + 1) * HALF)
                for j in range(CH):
                    last = mm(acc0[0:BM, hc], xp[:, j, :], cas[:, j, hc], j == 0, j == CH - 1)
            last.then_inc(s["freq_full"], 1)
            pe.wait_ge(s["freq_ready"], 1)
            fv = freq.rearrange("p (r j) -> p j r", j=CH)
            for j in range(CH):
                last = nc.tensor.transpose(acc1[:, j * BM:(j + 1) * BM], fv[:, j], ident[0:BM, 0:BM])
            last.then_inc(s["hart_full"], 1)
            pe.wait_ge(s["power_ready"], 1)
            pf = power[:].rearrange("p j m -> p (j m)")
            mm(acc0[:, 0:BM], flip[:, 0, :], pf[:, 0:BM], True, True)
            mm(acc0[:, BM:HALF], flip[:, 1, :], pf[:, BM:HALF], True, True).then_inc(s["flip_full"], 1)
            pe.wait_ge(s["msum_ready"], 1)
            for j in range(CH):
                last = mm(acc0[0:B, HALF:HALF + NBINS], msum[:, j, :], bins[:, j, :], j == 0, j == CH - 1)
            last.then_inc(s["energy_full"], 1)
            pe.wait_ge(s["sel_ready"], 1)
            nc.tensor.transpose(acc0[0:NBINS, 0:B], sel[5][:], ident[0:B, 0:B]).then_inc(s["selT_full"], 1)
            pe.wait_ge(s["selT_ready"], 1)
            for side in range(2):
                for j in range(CH):
                    o = HALF + (side * CH + j) * B
                    last = mm(acc1[:, o:o + B], regionb[:, side, j, :], selT[:], True, True)
            last.then_inc(s["enh_full"], 1)
            pe.wait_ge(s["coef_ready"], 1)
            for h in range(2):
                hc = slice(h * HALF, (h + 1) * HALF)
                for j in range(CH):
                    last = mm(acc0[0:BM, hc], coef[:, j, :], cas[:, j, hc], j == 0, j == CH - 1)
                last.then_inc(s["xe_full"], 1)
            for b in range(B):
                t = (acc1, tile[0], tile[1], acc0)[b]
                for h in range(2):
                    hc = slice(h * HALF, (h + 1) * HALF)
                    pe.wait_ge(s["xe_ready"], 2 if b == B - 1 else h + 1)
                    last = mm(t[:, hc], woutT[:, b, :], xe[:, hc], True, True)
                last.then_inc(s["y_full"], 1)

        @block.scalar
        def _(act):
            act.wait_ge(s["small_dve"], 1)
            nc.scalar.activation(std[:], var[:], ACT.Sqrt).then_inc(s["std_ready"], 1)
            act.preload_act_table_set("natural_log_exp_and_others")
            for ph in phases(act):
                a, b = ph.a, ph.b

                def take(step):
                    act.wait_ge(tile_full[ph.slot(step)], ph.filled(step))
                    return slots[ph.slot(step)]

                for step in ph.schedule:
                    name, i = step
                    if name == "fold":
                        t = take(step)
                        nc.scalar.activation(wT[:].rearrange("p k c -> p (k c)"), t[:, 0:5 * P],
                                             ACT.Copy).then_inc(s["wT_ready"], 1)
                    elif name == "gap":
                        t = take(step)
                        nc.scalar.activation(gapT[:], t[0:POOL * POOL, 0:P], ACT.Relu,
                                             scale=float(POOL * POOL) / N).then_inc(s["gapT_ready"], 1)
                    elif name == "gate":
                        t = take(step)
                        nc.scalar.activation(gate_h[:], t[:, 0:P], ACT.Copy).then_inc(s["gate_h_ready"], 1)
                    elif name == "val0":
                        t = take(step)
                        wait_past(act, s["v0n_ready"], a * CH)
                        nc.scalar.activation(v0[:].rearrange("p u c -> p (u c)"), t[:, :],
                                             ACT.Copy).then_inc(s["v0_ready"], 1)
                    elif name == "gram":
                        t = take(step)
                        act.wait_ge(s["nmax0_ready"], a * CH + i + 1)
                        wait_past(act, s["e0_used"], a * CH + max(i - RING + 1, 0))
                        nc.scalar.activation(e0[:, i % RING, :], t[:, :], ACT.Exp, bias=nmax0[:, i:i + 1],
                                             accum_out=sum0[:, i:i + 1]).then_inc(s["e0_ready"], 1)
                    elif name in ("qproj", "kproj"):
                        k = Q if name == "qproj" else K
                        t = take(step)
                        act.wait_ge(s["bias_ready"], 1)
                        if k == Q:
                            wait_past(act, s["qs2_ready"], 2 * b)
                        nc.scalar.activation((qs if k == Q else ks)[:], t[0:KS3, :], ACT.Identity,
                                             bias=bias[0:KS3, k:k + 1]).then_inc(s["hi_ready"], 1)
                    elif name in ("aproj", "sproj"):
                        k = A_ if name == "aproj" else S_
                        t = take(step)
                        if k == A_:
                            act.wait_ge(s["e1_ready"], (b + 1) * CH)
                        nc.scalar.activation((qs if k == A_ else ks)[:], t[0:KS3, :], ACT.Relu,
                                             bias=bias[0:KS3, k:k + 1]).then_inc(s["hi_ready"], 1)
                    elif name == "val1":
                        t = take(step)
                        wait_past(act, s["e1_used"], b * CH)
                        nc.scalar.activation(v1[:].rearrange("p u c -> p (u c)"), t[:, :],
                                             ACT.Copy).then_inc(s["v1_ready"], 1)
                    elif name == "score":
                        t = take(step)
                        act.wait_ge(s["nmax1_ready"], b * (CH + 2) + i + 1)
                        wait_past(act, s["sum1_ready"], b * 2 * CH + i - 1)
                        nc.scalar.activation(junk[:, i % 2, :], t[:, :], ACT.Exp, bias=nmax1[:, i:i + 1],
                                             accum_out=sum1[:, i:i + 1]).then_inc(s["sum1_ready"], 1)
                    elif name in ("shift1", "shift2"):
                        r = 1 if name == "shift1" else 2
                        act.wait_ge(s["sum1_ready"], b * 2 * CH + CH * r)
                        nc.scalar.activation(log1[:], sum1[:], ACT.Ln).then_inc(s["log1_ready"], 1)
                    elif name == "scoreT":
                        t = take(step)
                        wait_past(act, s["e1_used"], b * CH + max(i - RING + 1, 0))
                        nc.scalar.activation(e1[:, i % RING, :], t[:, :], ACT.Exp).then_inc(s["e1_ready"], 1)
                    elif name == "x2T":
                        t = take(step)
                        wait_past(act, s["acc1_full"], b)
                        nc.scalar.activation(x2T[:].rearrange("p u c -> p (u c)"), t[:, :],
                                             ACT.Copy).then_inc(s["x2T_ready"], 1)
                    elif name == "xkeep":
                        act.wait_ge(s["x2_ready"], b + 1)
                        wait_past(act, s["x3s_ready"], b)
                        nc.scalar.activation(xkeep[:], x2[:], ACT.Identity, scale=keep[:], bias=ngama[:]
                                             ).then_inc(s["xkeep_ready"], 1)
                    elif name == "chan":
                        t = take(step)
                        act.wait_ge(s["nmaxc_ready"], b + 1)
                        nc.scalar.activation(ec[:], t[:, 0:P], ACT.Exp, bias=nmaxc[:], accum_out=sumc[:]
                                             ).then_inc(s["ec_ready"], 1)
                    elif name == "chanT":
                        t = take(step)
                        nc.scalar.activation(ecT[:], t[:, 0:P], ACT.Copy).then_inc(s["ecT_ready"], 1)
                    elif name == "near":
                        t = take(step)
                        act.wait_ge(s["nmax1_ready"], b * (CH + 2) + CH + i + 1)
                        act.wait_ge(s["sum1_ready"], b * 2 * CH + CH + 4 * i)
                        if i == 0:
                            act.wait_ge(s["shf_ready"], 2 * b + 1)
                        for u in range(4 * i, 4 * i + 4):
                            nc.scalar.activation(junk[:, i, (u % 4) * WPAD:(u % 4) * WPAD + WIN], t[:, (u % 4) * WPAD:(u % 4) * WPAD + WIN], ACT.Exp,
                                                 bias=nmax1[:, u:u + 1], accum_out=sum1[:, u:u + 1]
                                                 ).then_inc(s["sum1_ready"], 1)
                    elif name == "nearT":
                        t = take(step)
                        tv = t[:, :].rearrange("p (u w) -> p u w", w=WPAD)[:, :, 0:WIN]
                        nc.scalar.activation(e2[:, 4 * i:4 * i + 4, :], tv, ACT.Exp).then_inc(s["e2_ready"], 1)
                    elif name == "x3":
                        act.wait_ge(s["zneg_ready"], b + 1)
                        nc.scalar.activation(zexp[:], zneg[:], ACT.Exp).then_inc(s["zexp_ready"], 1)

            act.wait_ge(s["freq_full"], 1)
            nc.scalar.activation(freq, acc0[0:BM, :], ACT.Copy).then_inc(s["freq_ready"], 1)
            act.wait_ge(s["hart_full"], 1)
            nc.scalar.activation(power[:].rearrange("p j m -> p (j m)"), acc1[:, 0:HALF],
                                 ACT.Square).then_inc(s["power_ready"], 1)
            nc.scalar.activation(hart[:].rearrange("p j m -> p (j m)"), acc1[:, 0:HALF],
                                 ACT.Copy).then_inc(s["hart_ready"], 1)
            act.wait_ge(s["both_ready"], CH)
            nc.scalar.activation(mag[:], both[:], ACT.Sqrt, scale=0.5).then_inc(s["mag_ready"], 1)
            act.wait_ge(s["selT_full"], 1)
            nc.scalar.activation(selT[:], acc0[0:NBINS, 0:B], ACT.Copy).then_inc(s["selT_ready"], 1)
            for h in range(2):
                act.wait_ge(s["xe_full"], h + 1)
                hc = slice(h * HALF, (h + 1) * HALF)
                nc.scalar.activation(xe[:, hc], acc0[0:BM, hc], ACT.Copy).then_inc(s["xe_ready"], 1)

        @block.vector
        def _(dve):
            vec = nc.vector
            def fold_bn():
                par = [rp[:, :, i] for i in range(6)]
                dve.wait_ge(s["weights_in"], 16 * 6)
                vec.tensor_scalar(var[:], par[4], EPS, None, ALU.add).then_inc(s["small_dve"], 1)
                dve.wait_ge(s["std_ready"], 1)
                small = [1]

                def link(ins):
                    small[0] += 1
                    ins.then_inc(s["small_dve"], 1)
                    dve.wait_ge(s["small_dve"], small[0])

                link(vec.reciprocal(rstd[:], std[:]))
                link(vec.tensor_tensor(nwt[:], rstd[:], rstd[:], ALU.mult))
                link(vec.tensor_tensor(nwt2[:], nwt[:], var[:], ALU.mult))
                link(vec.tensor_scalar(nwt3[:], nwt2[:], -0.5, 1.5, ALU.mult, ALU.add))
                link(vec.tensor_tensor(rstd2[:], rstd[:], nwt3[:], ALU.mult))
                link(vec.tensor_tensor(scale[:], rstd2[:], par[1], ALU.mult))
                link(vec.tensor_tensor(dev[:], par[0], par[3], ALU.subtract))
                link(vec.tensor_tensor(dev2[:], dev[:], scale[:], ALU.mult))
                link(vec.tensor_tensor(dev3[:], dev2[:], par[2], ALU.add))
                vec.tensor_tensor(bias[:], dev3[:], par[5], ALU.add).then_inc(s["bias_ready"], 1)
                link(vec.tensor_tensor(scale[:, V:V + 1], scale[:, V:V + 1], sc[:, 0:1], ALU.mult))
                link(vec.tensor_tensor(vb[:], dev3[:, V:V + 1], sc[:, 0:1], ALU.mult))
                link(vec.tensor_scalar(keep[:], sc[:, 1:2], -1.0, 1.0, ALU.mult, ALU.add))
                link(vec.tensor_scalar(ngama[:], sc[:, 1:2], -1.0, None, ALU.mult))
                for k in range(5):
                    vec.tensor_scalar(rws[:, k, :], rw[:, k, :], scale[:, k:k + 1], None,
                                      ALU.mult).then_inc(s["wfold_ready"], 1)
                
            for ph in phases(dve):
                a, b = ph.a, ph.b

                def take(step):
                    dve.wait_ge(tile_full[ph.slot(step)], ph.filled(step))
                    return slots[ph.slot(step)]

                for step in ph.schedule:
                    name, i = step
                    if name == "gate" and isinstance(a, int) and a == 0:
                        fold_bn()
                    if name == "split":
                        if isinstance(a, int) and a == 0:
                            dve.wait_ge(s["x_first_in"], 16)
                        else:
                            dve.wait_ge(s["x_rest_in"], 16 * (B - 1))
                            dve.wait_ge(s["e0_used"], a * CH)
                        xa = xin[:, a, :]
                        vec.tensor_copy(xh[:], xa).then_inc(s["xh_ready"], 1)
                        xv = xa.rearrange("p (y r x c) -> p y x r c", y=POOL, r=H // POOL, x=POOL)
                        vec.tensor_reduce(pooled[:].rearrange("p (y x) -> p y x", y=POOL), xv, AX.XY,
                                          ALU.add).then_inc(s["pooled_ready"], 1)
                    elif name == "gate":
                        t = take(step)
                        dve.wait_ge(s["gate_h_ready"], a + 1)
                        vec.tensor_tensor(gate_l[:], t[:, 0:P], gate_h[:].bitcast(F32),
                                          ALU.subtract).then_inc(s["gate_ready"], 1)
                    elif name == "gram":
                        t = take(step)
                        vec.tensor_reduce(nmax0[:, i:i + 1], t[:, :], AX.X, ALU.max,
                                          negate=True).then_inc(s["nmax0_ready"], 1)
                    elif name == "norm0":
                        dve.wait_ge(s["e0_ready"], a * CH + i + 1)
                        dve.wait_ge(s["v0_ready"], a + 1)
                        vec.reciprocal(rec0[:, i:i + 1], sum0[:, i:i + 1]).then_inc(s["rec0_ready"], 1)
                        dve.wait_ge(s["rec0_ready"], a * CH + i + 1)
                        vec.tensor_scalar(v0n[:, i, :], v0[:, i, :], rec0[:, i:i + 1], None,
                                          ALU.mult).then_inc(s["v0n_ready"], 1)
                    elif name == "x1":
                        dve.wait_ge(s["e0_used"], (a + 1) * CH)
                        vec.tensor_tensor(x1[:], acc0[:, :], xin[:, a, :], ALU.add).then_inc(s["x1_ready"], 1)
                    elif name in ("qproj", "kproj"):
                        k = Q if name == "qproj" else K
                        r = slice(2 * G, 3 * G) if k == Q else slice(G, 2 * G)
                        dst = (qs if k == Q else ks)[r, :]
                        t = take(step)
                        dve.wait_ge(s["hi_ready"], 4 * b + 1 + (k == K))
                        vec.scalar_tensor_tensor(out=dst, in0=t[r, :], scalar=bias[r, k:k + 1],
                                                 in1=dst.bitcast(F32), op0=ALU.add, op1=ALU.subtract
                                                 ).then_inc(s["q_ready" if k == Q else "k_ready"], 1)
                    elif name in ("aproj", "sproj"):
                        k = A_ if name == "aproj" else S_
                        r = slice(2 * G, 3 * G) if k == A_ else slice(G, 2 * G)
                        dst = (qs if k == A_ else ks)[r, :]
                        t = take(step)
                        dve.wait_ge(s["hi_ready"], 4 * b + 3 + (k == S_))
                        vec.tensor_scalar(full[r, k - A_, :], t[r, :], bias[r, k:k + 1], 0.0, ALU.add,
                                          ALU.max).then_inc(s["full_ready"], 1)
                        dve.wait_ge(s["full_ready"], 2 * b + 1 + (k == S_))
                        vec.tensor_tensor(dst, full[r, k - A_, :], dst.bitcast(F32), ALU.subtract
                                          ).then_inc(s["a_ready" if k == A_ else "s_ready"], 1)
                    elif name == "score":
                        t = take(step)
                        vec.tensor_reduce(nmax1[:, i:i + 1], t[:, :], AX.X, ALU.max,
                                          negate=True).then_inc(s["nmax1_ready"], 1)
                    elif name in ("shift1", "shift2"):
                        n = 2 * b + (1 if name == "shift1" else 2)
                        dve.wait_ge(s["log1_ready"], n)
                        vec.tensor_tensor(shf[:], nmax1[:], log1[:], ALU.subtract).then_inc(s["shf_ready"], 1)
                        dve.wait_ge(s["shf_ready"], n)
                        vec.tensor_copy(shf_h[:], shf[:]).then_inc(s["shf_h_ready"], 1)
                        dve.wait_ge(s["shf_h_ready"], n)
                        dve.wait_ge(s["diag_zero"], 1)
                        flat = diag[:].rearrange("p u c -> p (u c)")
                        d0 = flat[:, HID:HID + (CH - 1) * (P + 1) + 1:P + 1]
                        d2 = flat[:, 2 * G + HID:2 * G + HID + (CH - 1) * (P + 1) + 1:P + 1]
                        vec.tensor_copy(d0, shf_h[:].bitcast(F32))
                        vec.tensor_tensor(d2, shf[:], shf_h[:].bitcast(F32), ALU.subtract
                                          ).then_inc(s["diag_ready"], 1)
                        t = take(step)
                        vec.tensor_tensor(qs2[:], t[0:KS3, :], qs[:].bitcast(F32), ALU.add
                                          ).then_inc(s["qs2_ready"], 1)
                    elif name == "x2":
                        dve.wait_ge(s["e1_used"], (b + 1) * CH)
                        vec.scalar_tensor_tensor(out=x2[:], in0=acc1[:, :], scalar=vb[:], in1=x1[:],
                                                 op0=ALU.add, op1=ALU.add).then_inc(s["x2_ready"], 1)
                    elif name == "near":
                        t = take(step)
                        tv = t[:, :].rearrange("p (u w) -> p u w", w=WPAD)[:, :, 0:WIN]
                        vec.tensor_reduce(nmax1[:, 4 * i:4 * i + 4], tv, AX.X, ALU.max,
                                          negate=True).then_inc(s["nmax1_ready"], 1)
                    elif name == "chan":
                        t = take(step)
                        vec.tensor_reduce(nmaxc[:], t[:, 0:P], AX.X, ALU.max, negate=True
                                          ).then_inc(s["nmaxc_ready"], 1)
                        dve.wait_ge(s["ec_ready"], b + 1)
                        vec.reciprocal(recc[:], sumc[:]).then_inc(s["recc_ready"], 1)
                        dve.wait_ge(s["recc_ready"], b + 1)
                        vec.tensor_scalar(ecn[:], ec[:], recc[:], None, ALU.mult).then_inc(s["ecn_ready"], 1)
                    elif name == "x3":
                        dve.wait_ge(s["acc1_full"], b + 1)
                        vec.tensor_scalar(zneg[:], acc1[:, :], 0.0, None, ALU.min).then_inc(s["zneg_ready"], 1)
                        dve.wait_ge(s["zexp_ready"], b + 1)
                        vec.scalar_tensor_tensor(out=zelu[:], in0=acc1[:, :], scalar=0.0, in1=zexp[:],
                                                 op0=ALU.max, op1=ALU.add).then_inc(s["zelu_ready"], 1)
                        dve.wait_ge(s["zelu_ready"], b + 1)
                        dve.wait_ge(s["xkeep_ready"], b + 1)
                        wait_past(dve, s["x3_ready"], b)
                        vec.scalar_tensor_tensor(out=x3s[:], in0=zelu[:], scalar=sc[:, 1:2], in1=xkeep[:],
                                                 op0=ALU.mult, op1=ALU.add).then_inc(s["x3s_ready"], 1)
                    elif name == "xproj":
                        t = take(step)
                        vec.tensor_copy(xp[:, :, bass.ds(b * M, M)] if not isinstance(b, int)
                                        else xp[:, :, b * M:(b + 1) * M],
                                        t[:, 0:CH * M].rearrange("p (u m) -> p u m", m=M)
                                        ).then_inc(s["xp_ready"], 1)

            dve.wait_ge(s["flip_full"], 1)
            dve.wait_ge(s["power_ready"], 1)
            for j in range(CH):
                o = (CH - j) % CH * BM
                vec.tensor_tensor(both[:, j, :], acc0[:, o:o + BM], power[:, j, :], ALU.add).then_inc(s["both_ready"], 1)
            dve.wait_ge(s["mag_ready"], 1)
            vec.tensor_reduce(msum[:].rearrange("p j b -> p (j b)"), mag[:].rearrange("p j (b m) -> p (j b) m", m=M),
                              AX.X, ALU.add).then_inc(s["msum_ready"], 1)
            count = [0]

            def step(ins):
                count[0] += 1
                ins.then_inc(s["pick"], 1)
                dve.wait_ge(s["pick"], count[0])

            NB = NBINS
            e = es[:, 1:NB + 1]
            step(vec.memset(en[:], 0.0))
            dve.wait_ge(s["energy_full"], 1)
            step(vec.tensor_scalar(en[:, 1:NB + 1], acc0[0:B, HALF:HALF + NB], 1.0 / M, None, ALU.mult))
            step(vec.tensor_tensor(es_a[:], en[:, 0:NB], en[:, 2:NB + 2], ALU.add))
            step(vec.scalar_tensor_tensor(out=e, in0=en[:, 1:NB + 1], scalar=2.0, in1=es_a[:],
                                          op0=ALU.mult, op1=ALU.add, accum_out=one[:, 0:1]))
            vec.tensor_copy(es[:, 0:1], es[:, NB:NB + 1])
            vec.tensor_copy(es[:, NB + 1:NB + 2], es[:, 1:2])
            step(vec.tensor_scalar(one[:, 1:2], one[:, 0:1], 1.0 / NB, None, ALU.mult))
            step(vec.tensor_tensor(pk[0][:], es[:, 0:NB], es[:, 2:NB + 2], ALU.max))
            step(vec.tensor_tensor(pk[1][:], e, pk[0][:], ALU.is_gt))
            step(vec.scalar_tensor_tensor(out=pk[2][:], in0=e, scalar=one[:, 1:2], in1=pk[1][:],
                                          op0=ALU.is_gt, op1=ALU.mult))
            step(vec.tensor_tensor(pk[0][:], pk[2][:], e, ALU.mult))
            step(vec.tensor_reduce(one[:, 2:3], pk[0][:], AX.X, ALU.max))
            step(vec.tensor_scalar(one[:, 3:4], one[:, 2:3], 0.0, None, ALU.is_equal))
            step(vec.scalar_tensor_tensor(out=pk[1][:], in0=e, scalar=one[:, 3:4], in1=pk[0][:],
                                          op0=ALU.mult, op1=ALU.max))
            dve.wait_ge(s["masks_ready"], 6)

            def lowest_of_max(vals, top, key, low):
                step(vec.tensor_reduce(top, vals, AX.X, ALU.max))
                step(vec.scalar_tensor_tensor(out=key, in0=vals, scalar=top, in1=ramp[:],
                                              op0=ALU.is_equal, op1=ALU.mult))
                step(vec.tensor_reduce(low, key, AX.X, ALU.min))

            lowest_of_max(pk[1][:], one[:, 4:5], sel[0][:], one[:, 5:6])
            step(vec.scalar_tensor_tensor(out=sel[1][:], in0=ramp[:], scalar=one[:, 5:6], in1=pk[0][:],
                                          op0=ALU.not_equal, op1=ALU.mult))
            lowest_of_max(sel[1][:], one[:, 6:7], sel[2][:], one[:, 7:8])
            vec.tensor_scalar(sel[3][:], ramp[:], one[:, 5:6], None, ALU.is_equal)
            vec.tensor_scalar(one[:, 3:4], one[:, 6:7], 0.0, None, ALU.is_gt)
            step(vec.tensor_scalar(sel[4][:], ramp[:], one[:, 7:8], None, ALU.is_equal))
            vec.scalar_tensor_tensor(out=sel[5][:], in0=sel[4][:], scalar=one[:, 3:4], in1=sel[3][:],
                                     op0=ALU.mult, op1=ALU.add).then_inc(s["sel_ready"], 1)
            dve.wait_ge(s["enh_full"], 1)
            vec.tensor_scalar(enh[:].rearrange("p s j b -> p (s j b)"), acc1[:, HALF:HALF + 2 * CH * B],
                              1.0, None, ALU.min).then_inc(s["enh_chain"], 1)
            dve.wait_ge(s["enh_chain"], 1)
            vec.tensor_tensor(enh2[:], enh[:, 0], enh[:, 1], ALU.add).then_inc(s["enh_chain"], 1)
            dve.wait_ge(s["enh_chain"], 2)
            vec.tensor_tensor(gain[:], enh2[:], gains[:, :, 1:2].to_broadcast([P, CH, B]), ALU.mult
                              ).then_inc(s["enh_chain"], 1)
            dve.wait_ge(s["enh_chain"], 3)
            vec.tensor_tensor(enh2[:], gain[:], gains[:, :, 0:1].to_broadcast([P, CH, B]), ALU.add
                              ).then_inc(s["enh_chain"], 1)
            dve.wait_ge(s["enh_chain"], 4)
            dve.wait_ge(s["hart_ready"], 1)
            e2v = enh2[:].rearrange("p j b -> p (j b)").unsqueeze(2).to_broadcast([P, CH * B, M])
            vec.tensor_tensor(coef[:].rearrange("p j (b m) -> p (j b) m", m=M),
                              hart[:].rearrange("p j (b m) -> p (j b) m", m=M), e2v, ALU.mult
                              ).then_inc(s["coef_ready"], 1)
            for b in range(B):
                t = (acc1, tile[0], tile[1], acc0)[b]
                dve.wait_ge(s["y_full"], b + 1)
                dve.wait_ge(s["x3_ready"], B)
                vec.tensor_tensor(yout[:, b, :], t[:, :], x3[:, b, :], ALU.add).then_inc(s["y_ready"], 1)

        @block.gpsimd
        def _(pool):
            gp = nc.gpsimd
            gp.memset(diag[:], 0.0).then_inc(s["diag_zero"], 1)
            def constants():
                pool.wait_ge(s["weights_in"], 16 * 6)
                pool.wait_ge(s["const_in"], 16 * 3)
                gp.tensor_copy(identb[:], ident[:]).then_inc(s["masks_ready"], 1)
                gp.tensor_copy(nearb[:], near[:]).then_inc(s["masks_ready"], 1)
                gp.tensor_copy(chainb[:], chain[:]).then_inc(s["masks_ready"], 1)
                for side in range(2):
                    pool.wait_ge(s["region_in"], 16 * (side + 1))
                    gp.tensor_copy(regionb[:, side], region).then_inc(s["masks_ready"], 1)
                gp.iota(ramp[:], pattern=[[1, NBINS]], base=-NBINS, channel_multiplier=0,
                        allow_small_or_imprecise_dtypes=True).then_inc(s["masks_ready"], 1)

            for ph in phases(pool):
                b = ph.b
                for step in ph.schedule:
                    name, i = step
                    if name == "split":
                        pool.wait_ge(s["xh_ready"], ph.a + 1)
                        gp.tensor_tensor(xl[:], xin[:, ph.a, :], xh[:].bitcast(F32), ALU.subtract
                                         ).then_inc(s["xl_ready"], 1)
                    elif name == "gap" and isinstance(ph.a, int) and ph.a == 0:
                        constants()
                    elif name == "x3":
                        pool.wait_ge(s["x3s_ready"], b + 1)
                        gp.tensor_copy(x3[:, b, :], x3s[:]).then_inc(s["x3_ready"], 1)


def _tables():
    f = np.float32
    idx = np.arange(N)
    kh, kw = idx // W, idx % W
    turn = (np.outer(kh, kh) + np.outer(kw, kw)) % H
    ang = 2 * np.pi * np.arange(H) / H
    cas = ((np.cos(ang) + np.sin(ang)) / H)[turn].astype(f)
    order = idx.reshape(P, CH).T
    cas = np.ascontiguousarray(cas[order].transpose(1, 0, 2))
    neg = ((-kh) % H) * W + (-kw) % W
    where = np.empty(N, int)
    where[order.ravel()] = np.arange(N) % P
    flip = np.zeros((P, 2, P), f)
    for kind, j in ((0, 0), (1, 1)):
        for p in range(P):
            flip[where[neg[order[j, p]]], kind, p] = 1
    pi = f(np.pi)
    y, xx = ((kh + H // 2) % H).astype(f), ((kw + W // 2) % W).astype(f)
    r = np.sqrt((y - H // 2) ** 2 + (xx - W // 2) ** 2)
    theta = (np.arctan2((y - f(H // 2)).astype(float), xx - f(W // 2)).astype(f) + pi).astype(f)
    high = (r > f(0.3 * (H // 2))).astype(f)
    edges = _edges()
    mod = np.mod(theta, pi).astype(f)
    bin_of = np.clip(np.searchsorted(edges, mod, side="left") - 1, 0, NBINS - 1)
    onehot = np.zeros((N, NBINS), f)
    onehot[idx, bin_of] = high
    bins = np.ascontiguousarray(onehot[order].transpose(1, 0, 2))
    centre = ((edges[:-1] + edges[1:]) * f(0.5)).astype(f)
    diff = np.abs(theta[None] - centre[:, None])
    diff = np.minimum(diff, pi - diff)
    inside = ((diff <= f(np.radians(15.0))) & (high[None] > 0)).astype(f)
    region = np.stack([inside[:, order], inside[:, neg[order]]], 1)
    assert (high == high[neg]).all()
    gains = np.stack([np.where(high > 0, f(0.8), f(1.0)), f(0.2) * high], -1).astype(f)[order].transpose(1, 0, 2)
    n, m = np.arange(P), np.arange(WIN)
    di = np.abs((n // W + 1)[:, None] - (m // W)[None])
    dj = np.abs((n % W)[:, None] - (m % W)[None])
    adj = (di <= 1) & (dj <= 1) & ~((di == 0) & (dj == 0))
    near = np.full((P, 3, WIN), -9e15, f)
    for kind, ok in enumerate((m >= 0, m >= W, m < WIN - W)):
        near[:, kind][adj & ok[None]] = 0
    c = np.arange(C)
    chain = np.where(np.abs(c[:, None] - c[None]) == 1, f(0), f(-9e15)).astype(f)
    return dict(ident_in=np.eye(P, dtype=f), near_in=near, chain_in=chain, flip_in=flip, cas_in=cas, bins_in=bins,
                region_in=np.ascontiguousarray(region), gains_in=np.ascontiguousarray(gains))


def _edges():
    f = np.float32
    inner = np.arange(NBINS, dtype=f) * (f(1) / f(NBINS) * f(np.pi))
    return np.concatenate([inner, np.array([np.pi], f)])


def _pack(i):
    f = np.float32
    rows_w, rows_p = np.zeros((P, 5, P), f), np.zeros((P, 5, 6), f)
    keys = {Q: "L1_conv_q_", K: "L1_conv_k_", V: "L1_conv_v_"}
    for k, pre in keys.items():
        for g in ([0] if k == V else range(3)):
            at = slice(0, P) if k == V else slice(g * G, g * G + HID)
            rows_w[at, k] = i[pre + "w"]
            for n, part in enumerate(("b", "g", "beta", "mean", "var")):
                rows_p[at, k, n] = i[pre + part]
    for k, t in ((A_, "a"), (S_, "s")):
        for g in range(3):
            at = slice(g * G, g * G + HID)
            rows_w[at, k] = i[f"L2_conv_w{t}"]
            for n, part in ((1, "g"), (2, "b"), (3, "m"), (4, "v")):
                rows_p[at, k, n] = i[f"L2_conv_{part}{t}"]
    for g in range(3):
        for k in (K, S_):
            rows_p[g * G + HID:g * G + HID + CH, k, 5] = 1
    return rows_w, rows_p


def kernel(**inputs):
    import numpy as _np
    import concourse.bacc as _bacc
    from concourse import mybir as _mybir
    from concourse.bass_utils import run_bass_kernel_spmd as _run

    i = {k: _np.asarray(v) for k, v in inputs.items()}
    rows_w, rows_p = _pack(i)
    wout = _np.zeros((BM, B, P), _np.float32)
    for b in range(B):
        wout[b * M:(b + 1) * M, b] = i["L3_conv_w_out"].T
    scal = _np.zeros((P, 2), _np.float32)
    scal[:, 0] = i["L1_conv_gamma"][0]
    scal[:, 1] = i["L2_conv_gama"][0]
    data = dict(x=i["x"].reshape(B, C, N), rows_w=rows_w, rows_p=rows_p, scal=scal, wg_t=i["L0_conv_w_gap"].T,
                w_conv=i["L0_conv_w_conv"], win_t=i["L3_conv_w_in"].T, wout_t=wout, **_tables())
    nc = _bacc.Bacc("TRN2", target_bir_lowering=False, num_devices=1)
    arrays, args = {}, {}
    for name, v in data.items():
        v = _np.ascontiguousarray(v)
        arrays["in_" + name] = v
        args[name] = nc.dram_tensor("in_" + name, v.shape, _mybir.dt.from_np(v.dtype), kind="ExternalInput").ap()
    args["out"] = nc.dram_tensor("out_0", (B, C, N), _mybir.dt.float32, kind="ExternalOutput").ap()
    conv_seq(nc, **args)
    r = _run(nc, [arrays], core_ids=[0])
    return r.results[0]["out_0"].reshape(B, C, H, W)
```

```python
from contextlib import ExitStack

import numpy as np
import concourse.bass as bass
from concourse import mybir

ALU = mybir.AluOpType
ACT = mybir.ActivationFunctionType
AX = mybir.AxisListType
F32 = mybir.dt.float32
F32R = mybir.dt.float32r
BF16 = mybir.dt.bfloat16

P = 128
B, C, H, W = 4, 128, 32, 32
N = H * W
HALF = N // 2
CH = N // P
POOL = 8
HID = C // 8
G = 32
KS3 = 3 * G
WIN = P + 2 * W
WPAD = 256
M = 16
BM = B * M
NBINS = 90
EPS = 1e-5
QK, AS, V = range(3)

RING0 = 4
STAGE = 2
RING = 3

def steps(text):
    return [(w.split(":")[0], int(w.split(":")[1]) if ":" in w else 0) for w in text.split()]


L0_ALL = steps(
    "split pool gap gram:0 gate gram:1 gram:2 val0 norm0:0 gram:3 norm0:1 norm0:2 gram:4 norm0:3 mix:0 "
    "gram:5 mix:1 gram:6 norm0:4 mix:2 norm0:5 norm0:6 gram:7 mix:3 norm0:7 mix:4 mix:5 mix:6 bn mix:7 "
    "fold x1:0 x1:1")
ENDING = "join elu zelu x3 xproj".split()
STEADY = steps(
    "qkproj:0 split pool qkproj:1 join qklow:0 elu:0 qklow:1 elu:1 zelu:0 zelu:1 gap x3:0 val1 gate "
    "gram:0 score:0 val0 x3:1 score:1 score:2 gram:1 score:3 score:4 xproj score:5 norm0:0 gram:2 score:6 "
    "gram:3 score:7 norm0:1 mix:0 mix:1 shift1 norm0:2 norm0:3 scoreT:0 scoreT:1 e1h:0 gram:4 scoreT:2 "
    "e1l:0 e1h:1 e1l:1 mix:2 scoreT:3 gram:5 e1h:2 attend:0 attend:1 scoreT:4 e1h:3 scoreT:5 attend:2 "
    "e1l:2 e1l:3 attend:3 scoreT:6 e1h:4 e1l:4 e1h:5 e1l:5 e1h:6 attend:4 e1l:6 e1h:7 e1l:7 scoreT:7 "
    "attend:5 gram:6 attend:6 attend:7 x2:0 mix:3 x2:1 norm0:4 norm0:5 asproj:0 asproj:1 aslow:0 norm0:6 "
    "x2T mix:4 aslow:1 gram:7 near:0 near:1 mix:5 norm0:7 mix:6 mix:7 shift2 x1:0 xkeep chan nearT:0 "
    "nearT:1 x1:1 chanT")
START = [x for x in STEADY if x[0] not in ENDING]
L12_ALL = steps(
    "qkproj:0 qkproj:1 qklow:0 join elu:0 qklow:1 elu:1 zelu:0 zelu:1 score:0 score:1 score:2 score:3 "
    "score:4 score:5 score:6 score:7 shift1 val1 scoreT:0 e1h:0 e1l:0 e1h:1 e1l:1 scoreT:1 scoreT:2 "
    "attend:0 scoreT:3 scoreT:4 e1h:2 x3:0 e1h:3 attend:1 e1l:2 e1l:3 e1h:4 scoreT:5 attend:2 attend:3 "
    "e1l:4 scoreT:6 e1h:5 x3:1 scoreT:7 e1h:6 attend:4 e1l:5 e1l:6 xproj e1h:7 attend:5 attend:6 attend:7 "
    "e1l:7 x2:0 x2:1 asproj:0 asproj:1 aslow:0 x2T aslow:1 near:0 near:1 shift2 chan nearT:0 nearT:1 "
    "xkeep chanT")
END = steps(
    "join elu:0 elu:1 zelu:0 zelu:1 x3:0 x3:1 xproj")

ACC1, ACC0 = 2, 3
LAST_READER = {"fold": ("wT_ready", "a", 1, lambda i: 1),
               "gap": ("gapT_ready", "a", 1, lambda i: 1), "gate": ("gate_ready", "a", 1, lambda i: 1),
               "val0": ("v0_ready", "a", 1, lambda i: 1), "gram": ("e0_ready", "a", CH, lambda i: i + 1),
               "qkproj": ("full_ready", "b", 4, lambda i: i + 1), "val1": ("v1_ready", "b", 1, lambda i: 1),
               "score": ("sum1_ready", "b", 2 * CH, lambda i: i + 1),
               "shift1": ("qs2_ready", "b", 2, lambda i: 1), "shift2": ("qs2_ready", "b", 2, lambda i: 2),
               "scoreT": ("e1_ready", "b", CH, lambda i: i + 1), "asproj": ("full_ready", "b", 4, lambda i: i + 3),
               "x2T": ("x2T_ready", "b", 1, lambda i: 1),
               "chan": ("ec_ready", "b", 1, lambda i: 1), "chanT": ("ecT_ready", "b", 1, lambda i: 1),
               "near": ("sum1_ready", "b", 2 * CH, lambda i: CH + 4 * i + 4),
               "nearT": ("e2_ready", "b", 2, lambda i: i + 1),
               "attend": ("x2_ready", "b", 2, lambda i: 2), "join": ("zelu_ready", "b", 2, lambda i: 0),
               "xproj": ("xp_ready", "b", 1, lambda i: 0)}


class Plan:

    def __init__(self, schedule, like=None):
        self.schedule, self.slot, self.nth, self.prior = schedule, {}, {}, {}
        self.fills, self.last = [0] * 4, [None] * 4
        age, held, spare = [0, 1, 2, 0], False, False
        for at, step in enumerate(schedule):
            name, i = step
            if step in (("x2", 1), ("zelu", 1)):
                held = False
            if name == "xproj" and ("mix", 0) not in schedule:
                self.last[ACC0], spare = step, True
            accumulates = name == "join" or step == ("attend", 0)
            if name not in LAST_READER or name == "xproj" or (name == "attend" and i):
                continue
            if accumulates:
                slot, held = ACC1, True
            else:
                slot = like.slot[step] if like else min((0, 1) + (ACC1,) * (not held) + (ACC0,) * spare,
                                                               key=lambda k: age[k])
            self.slot[step], self.prior[step] = slot, self.last[slot]
            age[slot], self.last[slot] = at + 3, step
            if not accumulates:
                self.nth[step] = self.fills[slot]
                self.fills[slot] += 1


FIRST_PLAN, STEADY_PLAN, LAST_PLAN, END_PLAN = Plan(L0_ALL), Plan(STEADY), Plan(L12_ALL), Plan(END)
START_PLAN = Plan(START, STEADY_PLAN)


class Phase:

    def __init__(self, plan, a, b, turns=0, before=None):
        self.plan, self.a, self.b, self.turns, self.before = plan, a, b, turns, before
        self.schedule = plan.schedule
        self.c = None if b is None else b - 1

    def slot(self, step):
        return self.plan.slot[step]

    def filled(self, step):
        k = self.plan.slot[step]
        base = 0 if self.before is None else FIRST_PLAN.fills[k]
        return base + self.turns * STEADY_PLAN.fills[k] + self.plan.nth[step] + 1

    def freed(self, step):
        a, b, prior = self.a, self.b, self.plan.prior[step]
        if prior is None:
            if self.before is None:
                return None, 0
            prior = self.before.last[self.plan.slot[step]]
            a = self.b if self.a is None else self.a - 1
            b = None if self.b is None else self.b - 1
            if prior is None:
                return None, 0
        name, i = prior
        sem, which, per_image, at = LAST_READER[name]
        return sem, (a if which == "a" else b) * per_image + at(i)


def phases(engine):
    yield Phase(FIRST_PLAN, 0, None)
    yield Phase(START_PLAN, 1, 0, 0, FIRST_PLAN)
    with engine.Fori(1, B - 1) as t:
        yield Phase(STEADY_PLAN, t + 1, t, t, STEADY_PLAN)
    yield Phase(LAST_PLAN, None, B - 1, B - 1, STEADY_PLAN)
    yield Phase(END_PLAN, None, B, B - 1, LAST_PLAN)


def wait_past(engine, sem, count):
    if not (isinstance(count, int) and count <= 0):
        engine.wait_ge(sem, count)


def conv_seq(nc, x, rows_w, rows_p, scal, wg_t, w_conv, win_t, wout_t, ident_in, near_in, chain_in,
             fold_in, flip_in, cas_h_in, cas_l_in, bins_in, region_in, gains_in, out):
    with ExitStack() as ctx:
        def sb(name, shape, dt=F32):
            return ctx.enter_context(nc.sbuf_tensor(name, shape, dt))

        def sem(name):
            return ctx.enter_context(nc.semaphore(name))

        tile = [ctx.enter_context(nc.psum_tensor(f"tile{i}", [P, N], F32)) for i in range(2)]
        acc0 = ctx.enter_context(nc.psum_tensor("acc0", [P, N], F32))
        acc1 = ctx.enter_context(nc.psum_tensor("acc1", [P, N], F32))
        slots = (tile[0], tile[1], acc1, acc0)

        rw = sb("rw", [P, 3, P])
        rp = sb("rp", [P, 3, 6])
        sc = sb("sc", [P, 2])
        wgT = sb("wgT", [P, P])
        wc = sb("wc", [POOL * POOL, P])
        winT = sb("winT", [P, M])
        woutT = sb("woutT", [2 * BM, B, P])
        ident = sb("ident", [P, P])
        chain = sb("chain", [P, P])
        flip = sb("flip", [P, 2, P])
        fold2 = sb("fold2", [2 * BM, BM])
        bins = sb("bins", [P, CH, NBINS + 3])
        gains = sb("gains", [P, CH, 2])
        identb = sb("identb", [P, P], BF16)
        nearb = sb("nearb", [P, 3, WIN], BF16)
        chainb = sb("chainb", [P, P], BF16)
        std = sb("std", [P, 3])
        var = sb("var", [P, 3])
        rstd = sb("rstd", [P, 3])
        nwt = sb("nwt", [P, 3])
        nwt2 = sb("nwt2", [P, 3])
        nwt3 = sb("nwt3", [P, 3])
        rstd2 = sb("rstd2", [P, 3])
        scale = sb("scale", [P, 3])
        dev = sb("dev", [P, 3])
        dev2 = sb("dev2", [P, 3])
        dev3 = sb("dev3", [P, 3])
        bias = sb("bias", [P, 3])
        vb = sb("vb", [P, 1])
        keep = sb("keep", [P, 1])
        ngama = sb("ngama", [P, 1])
        rws = sb("rws", [P, 3, P])
        wT = sb("wT", [P, 3, P])

        xin = sb("xin", [P, B, N])
        x1 = sb("x1", [P, N])
        with ExitStack() as l0_only:
            def sb0(name, shape, dt=F32):
                return l0_only.enter_context(nc.sbuf_tensor(name, shape, dt))

            xs = sb0("xs", [P, N])
            xh = sb0("xh", [P, N], F32R)
            xl = sb0("xl", [P, N], F32R)
            v0 = sb0("v0", [P, CH, P])
            v0n = sb0("v0n", [P, CH, P])
            e0 = sb0("e0", [P, RING0, N])
        cas_h = sb("cas_h", [P, CH, N], F32R)
        cas_l = sb("cas_l", [P, CH, N], F32R)
        pooled = sb("pooled", [P, POOL * POOL])
        gapT = sb("gapT", [POOL * POOL, P])
        gate = sb("gate", [P, P])
        nmax0 = sb("nmax0", [P, CH])
        sum0 = sb("sum0", [P, CH])
        rec0 = sb("rec0", [P, CH])
        qs = sb("qs", [KS3, N], F32R)
        ks = sb("ks", [KS3, N], F32R)
        qs2 = sb("qs2", [KS3, N], F32R)
        full = sb("full", [P, N])
        v1h = sb("v1h", [P, CH, P], F32R)
        v1l = sb("v1l", [P, CH, P], F32R)
        nmax1 = sb("nmax1", [P, CH])
        sum1 = sb("sum1", [P, CH])
        log1 = sb("log1", [P, CH])
        shf = sb("shf", [P, CH])
        shf_h = sb("shf_h", [P, CH], F32R)
        diag = sb("diag", [P, CH, P])
        with ExitStack() as l1_only:
            e1 = l1_only.enter_context(nc.sbuf_tensor("e1", [P, STAGE, N], F32))
            e1h = l1_only.enter_context(nc.sbuf_tensor("e1h", [P, RING, N], F32R))
            e1l = l1_only.enter_context(nc.sbuf_tensor("e1l", [P, RING, N], F32R))
        hart = sb("hart", [P, CH, BM])
        power = sb("power", [P, CH, BM])
        both = sb("both", [P, CH, BM])
        mag = sb("mag", [P, CH, BM])
        coef = sb("coef", [P, CH, BM])
        coef2 = sb("coef2", [P, CH, 2, BM], F32R)
        sb("l1_rest", [P, (STAGE + 2 * RING) * N - 7 * CH * BM])
        x2 = sb("x2", [P, N])
        x2T = sb("x2T", [P, CH, P])
        nmaxc = sb("nmaxc", [P, 1])
        sumc = sb("sumc", [P, 1])
        recc = sb("recc", [P, 1])
        ec = sb("ec", [P, P])
        ecn = sb("ecn", [P, P])
        ecT = sb("ecT", [P, P])
        e2 = sb("e2", [P, CH, WIN])
        xkeep = sb("xkeep", [P, N])
        zneg = sb("zneg", [P, N])
        zexp = sb("zexp", [P, N])
        zelu = zneg
        x3s = sb("x3s", [P, N])
        x3 = xin
        xp = sb("xp", [P, CH, 2, BM], F32R)
        msum = sb("msum", [P, CH, B])
        es = sb("es", [B, NBINS + 3])
        pk = [sb(f"pk{i}", [B, NBINS]) for i in range(4)]
        sel = [sb(f"sel{i}", [B, NBINS]) for i in range(6)]
        one = sb("one", [B, 8])
        ramp = sb("ramp", [B, NBINS])
        selT = sb("selT", [NBINS, B], BF16)
        freq = zneg[:, :]
        regionb = sb("regionb", [NBINS, 2, CH, P], BF16)
        enh = sb("enh", [P, 2, CH, B])
        enh2 = sb("enh2", [P, CH, B])
        gain = sb("gain", [P, CH, B])
        xe = zexp[:, :]
        yout = x3

        near = x3s[:, 0:3 * WIN].rearrange("p (k w) -> p k w", w=WIN)
        region = zexp[0:NBINS, :].rearrange("p (j c) -> p j c", c=P)
        tile_full = [sem(f"tile_full{i}") for i in range(4)]
        names = """x_first_in x_rest_in weights_in const_in cas_in cas_h_in cas_l_in std_ready
            small_dve bias_ready wfold_ready wT_ready
            masks_ready diag_zero
            xh_ready xl_ready pooled_ready gapT_ready gate_ready xs_ready v0_ready
            nmax0_ready e0_ready rec0_ready v0n_ready e0_used x1_ready
            full_ready hi_ready qhi_ready low_ready v1_ready nmax1_ready sum1_ready log1_ready shf_ready shf_h_ready diag_ready
            qs2_ready v1h_ready e1_ready e1h_ready e1l_ready e1_used acc1_full x2_ready
            x2T_ready nmaxc_ready ec_ready recc_ready ecn_ready ecT_ready e2_ready xkeep_ready
            zneg_ready zexp_ready zelu_ready x3s_ready x3_ready xproj_full xp_h_ready xp_ready
            freq_full freq_ready region_in hart_full hart_ready power_ready flip_full both_ready mag_ready msum_ready energy_full
            pick sel_ready selT_full selT_ready enh_full coef_ready enh_chain xe_full xe_ready
            y_full y_ready out_written""".split()
        s = {n: sem(n) for n in names}

        block = ctx.enter_context(nc.Block())

        @block.sync
        def _(sp):
            for b in range(B):
                sp.dma_start(xin[:, b, :], x[b]).then_inc(s["x_rest_in" if b else "x_first_in"], 16)
                if b == 0:
                    for dst, src in ((ident, ident_in), (wgT, wg_t), (wc, w_conv), (rp, rows_p), (rw, rows_w),
                                     (sc, scal)):
                        sp.dma_start(dst[:], src).then_inc(s["weights_in"], 16)
            for dst, src in ((near, near_in), (chain[:], chain_in), (winT[:], win_t)):
                sp.dma_start(dst, src).then_inc(s["const_in"], 16)
            for dst, src in ((woutT, wout_t), (fold2, fold_in), (flip, flip_in), (bins, bins_in), (gains, gains_in)):
                sp.dma_start(dst[:], src).then_inc(s["cas_in"], 16)
            for side in range(2):
                if side:
                    sp.wait_ge(s["masks_ready"], 4)
                sp.dma_start(region, region_in[:, side]).then_inc(s["region_in"], 16)
            for b in range(B - 1):
                sp.wait_ge(s["y_ready"], 2 * b + 2)
                sp.dma_start(out[b], yout[:, b, :]).then_inc(s["out_written"], 16)
            for h in range(2):
                hc = slice(h * HALF, (h + 1) * HALF)
                sp.wait_ge(s["y_ready"], 2 * B - 1 + h)
                sp.dma_start(out[B - 1][:, hc], yout[:, B - 1, hc]).then_inc(s["out_written"], 16)
            sp.wait_ge(s["out_written"], 16 * (B + 1))

        @block.tensor
        def _(pe):
            def mm(o, lhsT, rhs, start, stop, skip=False):
                return nc.tensor.matmul(o, lhsT, rhs, start=start, stop=stop, skip_group_check=skip)


            for ph in phases(pe):
                a, b, c = ph.a, ph.b, ph.c

                def begin(step, waited=None):
                    last_reader, count = ph.freed(step)
                    if last_reader and last_reader != waited:
                        pe.wait_ge(s[last_reader], count)
                    return slots[ph.slot(step)]

                def end(step, ins):
                    ins.then_inc(tile_full[ph.slot(step)], 1)

                for step in ph.schedule:
                    name, i = step
                    cols = slice(i * P, (i + 1) * P)
                    if name == "fold":
                        pe.wait_ge(s["wfold_ready"], 3)
                        t = begin(step)
                        for k in range(3):
                            last = nc.tensor.transpose(t[:, k * P:(k + 1) * P], rws[:, k, :], ident[:])
                        end(step, last)
                    elif name == "gap":
                        pe.wait_ge(s["pooled_ready"], a + 1)
                        if isinstance(a, int) and a == 0:
                            pe.wait_ge(s["weights_in"], 16 * 6)
                        t = begin(step)
                        end(step, mm(t[0:POOL * POOL, 0:P], pooled[:], wgT[:], True, True))
                    elif name == "gate":
                        pe.wait_ge(s["gapT_ready"], a + 1)
                        t = begin(step)
                        end(step, mm(t[:, 0:P], wc[:], gapT[:], True, True))
                    elif name == "val0":
                        pe.wait_ge(s["gate_ready"], a + 1)
                        pe.wait_ge(s["xs_ready"], a + 1)
                        t = begin(step)
                        for u in range(CH):
                            cu = slice(u * P, (u + 1) * P)
                            last = mm(t[:, cu], xs[:, cu], gate[:], True, True)
                        end(step, last)
                    elif name == "gram":
                        pe.wait_ge(s["xl_ready"], a + 1)
                        t = begin(step)
                        for h in range(2):
                            hc = slice(h * HALF, (h + 1) * HALF)
                            mm(t[:, hc], xh[:, cols], xh[:, hc], True, False)
                            mm(t[:, hc], xh[:, cols], xl[:, hc], False, False)
                            last = mm(t[:, hc], xl[:, cols], xh[:, hc], False, True)
                        end(step, last)
                    elif name == "mix":
                        pe.wait_ge(s["e0_ready"], a * CH + i + 1)
                        pe.wait_ge(s["v0n_ready"], a * CH + i + 1)
                        if i == 0:
                            wait_past(pe, s["x1_ready"], 2 * a)
                            wait_past(pe, s["xp_ready"], a - 1)
                        for h in range(2):
                            hc = slice(h * HALF, (h + 1) * HALF)
                            last = mm(acc0[:, hc], v0n[:, i, :], e0[:, i % RING0, hc], i == 0, i == CH - 1)
                        last.then_inc(s["e0_used"], 1)
                    elif name in ("qkproj", "asproj"):
                        k = QK if name == "qkproj" else AS
                        src = x1 if k == QK else x2
                        hc = slice(i * HALF, (i + 1) * HALF)
                        pe.wait_ge(s["x1_ready" if k == QK else "x2_ready"], 2 * b + i + 1)
                        if k == QK:
                            pe.wait_ge(s["wT_ready"], 1)
                        t = begin(step)
                        end(step, mm(t[:, 0:HALF], wT[:, k, :], src[:, hc], True, True))
                    elif name == "val1":
                        pe.wait_ge(s["x1_ready"], 2 * b + 2)
                        t = begin(step)
                        for u in range(CH):
                            cu = slice(u * P, (u + 1) * P)
                            last = mm(t[:, cu], x1[:, cu], wT[:, V, :], True, True)
                        end(step, last)
                    elif name == "score":
                        pe.wait_ge(s["hi_ready"], 8 * b + 4)
                        pe.wait_ge(s["low_ready"], 4 * b + 2)
                        t = begin(step)
                        for h in range(2):
                            hc = slice(h * HALF, (h + 1) * HALF)
                            last = mm(t[:, hc], qs[:, cols], ks[:, hc], True, True)
                        end(step, last)
                    elif name in ("shift1", "shift2"):
                        pe.wait_ge(s["diag_ready"], 2 * b + (1 if name == "shift1" else 2))
                        t = begin(step)
                        for u in range(CH):
                            last = nc.tensor.transpose(t[0:KS3, u * P:(u + 1) * P], diag[:, u, 0:KS3], ident[:])
                        end(step, last)
                    elif name == "scoreT":
                        pe.wait_ge(s["qs2_ready"], 2 * b + 1)
                        t = begin(step, "qs2_ready")
                        for h in range(2):
                            hc = slice(h * HALF, (h + 1) * HALF)
                            last = mm(t[:, hc], ks[:, cols], qs2[:, hc], True, True)
                        end(step, last)
                    elif name == "attend":
                        pe.wait_ge(s["e1h_ready"], b * CH + i + 1)
                        pe.wait_ge(s["v1_ready"], b + 1)
                        if i == 0:
                            begin(step)
                        for k, (vv, ee) in enumerate(((v1h, e1h), (v1l, e1h), (v1h, e1l))):
                            if k == 2:
                                pe.wait_ge(s["e1l_ready"], b * CH + i + 1)
                            for h in range(2):
                                hc = slice(h * HALF, (h + 1) * HALF)
                                last = mm(acc1[:, hc], vv[:, i, :], ee[:, i % RING, hc], i == 0 and k == 0,
                                          i == CH - 1 and k == 2)
                        last.then_inc(s["e1_used"], 1)
                    elif name == "x2T":
                        pe.wait_ge(s["x2_ready"], 2 * b + 2)
                        t = begin(step)
                        for u in range(CH):
                            cu = slice(u * P, (u + 1) * P)
                            last = nc.tensor.transpose(t[:, cu], x2[:, cu], ident[:])
                        end(step, last)
                    elif name == "chan":
                        pe.wait_ge(s["x2T_ready"], b + 1)
                        pe.wait_ge(s["masks_ready"], 3)
                        t = begin(step)
                        for u in range(CH):
                            mm(t[:, 0:P], x2T[:, u, :], x2T[:, u, :], u == 0, False)
                        end(step, mm(t[:, 0:P], identb[:], chainb[:], False, True))
                    elif name == "chanT":
                        pe.wait_ge(s["ecn_ready"], b + 1)
                        t = begin(step)
                        end(step, nc.tensor.transpose(t[:, 0:P], ecn[:], ident[:]))
                    elif name in ("near", "nearT"):
                        if name == "near":
                            pe.wait_ge(s["hi_ready"], 8 * b + 8)
                            pe.wait_ge(s["low_ready"], 4 * b + 4)
                            pe.wait_ge(s["masks_ready"], 3)
                            lhs, rhs = qs, ks
                        else:
                            pe.wait_ge(s["qs2_ready"], 2 * b + 2)
                            lhs, rhs = ks, qs2
                        t = begin(step, "qs2_ready")
                        for u in range(4 * i, 4 * i + 4):
                            kind = 1 if u == 0 else 2 if u == CH - 1 else 0
                            lo, hi = max(u * P - W, 0), min((u + 1) * P + W, N)
                            w0 = (u % 4) * WPAD
                            off = w0 + lo - (u * P - W)
                            first = u % 2 == 0
                            mm(t[:, w0:w0 + WIN], identb[:], nearb[:, kind, :], first, False, True)
                            last = mm(t[:, off:off + hi - lo], lhs[:, u * P:(u + 1) * P], rhs[:, lo:hi],
                                      False, not first, True)
                        end(step, last)
                    elif name == "join":
                        pe.wait_ge(s["ecT_ready"], c + 1)
                        pe.wait_ge(s["e2_ready"], 2 * c + 2)
                        begin(step, "e2_ready")
                        for h in range(2):
                            hc = slice(h * HALF, (h + 1) * HALF)
                            mm(acc1[:, hc], ecT[:], x2[:, hc], True, False, True)
                            for u in range(CH):
                                lo = max(u * P - W, h * HALF)
                                hi = min((u + 1) * P + W, (h + 1) * HALF)
                                if lo >= hi:
                                    continue
                                off = lo - (u * P - W)
                                last = mm(acc1[:, lo:hi], x2T[:, u, :], e2[:, u, off:off + hi - lo],
                                          False, u * P + P + W >= (h + 1) * HALF and u in (4, 7), True)
                            last.then_inc(s["acc1_full"], 1)
                    elif name == "xproj":
                        pe.wait_ge(s["x3s_ready"], 2 * c + 2)
                        pe.wait_ge(s["const_in"], 16 * 3)
                        x3v = x3s[:].rearrange("p (r j) -> p j r", j=CH)
                        for u in range(CH):
                            last = mm(acc0[:, u * M:(u + 1) * M], x3v[:, u], winT[:], True, True)
                        last.then_inc(s["xproj_full"], 1)

            pe.wait_ge(s["cas_in"], 16 * 5)
            pe.wait_ge(s["cas_l_in"], 16 * CH)
            pe.wait_ge(s["cas_h_in"], 16 * CH)
            pe.wait_ge(s["xp_ready"], B)

            def hartley(parts, full_sem, parts_ready=None):
                for h in range(2):
                    hc = slice(h * HALF, (h + 1) * HALF)
                    for j in range(CH):
                        if parts_ready and h == 0 and j % (CH // 2) == 0:
                            pe.wait_ge(parts_ready, j // (CH // 2) + 1)
                        mm(acc0[:, hc], parts[:, j].rearrange("p s m -> p (s m)"), cas_h[:, j, hc], j == 0, False, True)
                        last = mm(acc0[0:BM, hc], parts[:, j, 0, :], cas_l[:, j, hc], False, j == CH - 1, True)
                    last.then_inc(full_sem, 1)

            hartley(xp, s["freq_full"])
            pe.wait_ge(s["freq_ready"], 2)
            fv = freq.rearrange("p (r j) -> p j r", j=CH)
            for j in range(CH):
                last = mm(acc1[:, j * BM:(j + 1) * BM], fv[:, j], fold2[:], True, True)
            last.then_inc(s["hart_full"], 1)
            pe.wait_ge(s["power_ready"], 1)
            pf = power[:].rearrange("p j m -> p (j m)")
            mm(acc0[:, 0:BM], flip[:, 0, :], pf[:, 0:BM], True, True)
            mm(acc0[:, BM:HALF], flip[:, 1, :], pf[:, BM:HALF], True, True).then_inc(s["flip_full"], 1)
            for j in range(CH):
                if j % (CH // 2) == 0:
                    pe.wait_ge(s["msum_ready"], j // (CH // 2) + 1)
                last = mm(acc0[0:B, HALF:HALF + NBINS + 3], msum[:, j, :], bins[:, j, :], j == 0, j == CH - 1)
            last.then_inc(s["energy_full"], 1)
            pe.wait_ge(s["sel_ready"], 1)
            nc.tensor.transpose(acc0[0:NBINS, 0:B], sel[5][:], ident[0:B, 0:B]).then_inc(s["selT_full"], 1)
            pe.wait_ge(s["selT_ready"], 1)
            for side in range(2):
                for j in range(CH):
                    o = HALF + (side * CH + j) * B
                    last = mm(acc1[:, o:o + B], regionb[:, side, j, :], selT[:], True, True)
            last.then_inc(s["enh_full"], 1)
            hartley(coef2, s["xe_full"], s["coef_ready"])
            for b in range(B):
                t = (acc1, tile[0], tile[1], acc0)[b]
                for h in range(2):
                    hc = slice(h * HALF, (h + 1) * HALF)
                    pe.wait_ge(s["xe_ready"], 2 if b == B - 1 else h + 1)
                    mm(t[:, hc], woutT[:, b, :], xe[:, hc], True, True).then_inc(s["y_full"], 1)

        @block.scalar
        def _(act):
            for ph in phases(act):
                a, b, c = ph.a, ph.b, ph.c

                def take(step):
                    act.wait_ge(tile_full[ph.slot(step)], ph.filled(step))
                    return slots[ph.slot(step)]

                for step in ph.schedule:
                    name, i = step
                    if name == "bn":
                        act.wait_ge(s["small_dve"], 1)
                        nc.scalar.activation(std[:], var[:], ACT.Sqrt).then_inc(s["std_ready"], 1)
                        act.preload_act_table_set("natural_log_exp_and_others")
                    elif name == "fold":
                        t = take(step)
                        nc.scalar.activation(wT[:].rearrange("p k c -> p (k c)"), t[:, 0:3 * P],
                                             ACT.Copy).then_inc(s["wT_ready"], 1)
                    elif name == "gap":
                        t = take(step)
                        nc.scalar.activation(gapT[:], t[0:POOL * POOL, 0:P], ACT.Relu,
                                             scale=float(POOL * POOL) / N).then_inc(s["gapT_ready"], 1)
                    elif name == "gate":
                        t = take(step)
                        nc.scalar.activation(gate[:], t[:, 0:P], ACT.Copy).then_inc(s["gate_ready"], 1)
                    elif name == "split":
                        if isinstance(a, int) and a == 0:
                            act.wait_ge(s["x_first_in"], 16)
                        else:
                            act.wait_ge(s["x_rest_in"], 16 * (B - 1))
                        wait_past(act, s["v0_ready"], a)
                        nc.scalar.activation(xs[:], xin[:, a, :], ACT.Copy).then_inc(s["xs_ready"], 1)
                    elif name == "val0":
                        t = take(step)
                        wait_past(act, s["v0n_ready"], a * CH)
                        nc.scalar.activation(v0[:].rearrange("p u c -> p (u c)"), t[:, :],
                                             ACT.Copy).then_inc(s["v0_ready"], 1)
                    elif name == "gram":
                        t = take(step)
                        act.wait_ge(s["nmax0_ready"], a * CH + i + 1)
                        wait_past(act, s["e0_used"], a * CH + max(i - RING0 + 1, 0))
                        nc.scalar.activation(e0[:, i % RING0, :], t[:, :], ACT.Exp, bias=nmax0[:, i:i + 1],
                                             accum_out=sum0[:, i:i + 1]).then_inc(s["e0_ready"], 1)
                    elif name in ("qkproj", "asproj"):
                        t = take(step)
                        hc = slice(i * HALF, (i + 1) * HALF)
                        k, n = (QK, 4 * b + 1 + i) if name == "qkproj" else (AS, 4 * b + 3 + i)
                        if k == QK:
                            act.wait_ge(s["bias_ready"], 1)
                            wait_past(act, s["e2_ready"], 2 * b)
                        else:
                            act.wait_ge(s["e1_ready"], (b + 1) * CH)
                        wait_past(act, s["low_ready"], n - 2)
                        nc.scalar.activation(full[:, hc], t[:, 0:HALF], ACT.Identity if k == QK else ACT.Relu,
                                             bias=bias[:, k:k + 1]).then_inc(s["full_ready"], 1)
                        act.wait_ge(s["full_ready"], n)
                        nc.scalar.activation(ks[2 * G:3 * G, hc], full[2 * G:3 * G, hc], ACT.Copy
                                             ).then_inc(s["hi_ready"], 1)
                        nc.scalar.activation(ks[0:G, hc], full[3 * G:4 * G, hc], ACT.Copy
                                             ).then_inc(s["hi_ready"], 1)
                    elif name == "val1":
                        t = take(step)
                        wait_past(act, s["e1_used"], b * CH)
                        nc.scalar.activation(v1h[:].rearrange("p u c -> p (u c)"), t[:, :],
                                             ACT.Copy).then_inc(s["v1h_ready"], 1)
                    elif name == "score":
                        t = take(step)
                        act.wait_ge(s["nmax1_ready"], b * (CH + 2) + i + 1)
                        nc.scalar.activation(t[:, :], t[:, :], ACT.Exp, bias=nmax1[:, i:i + 1],
                                             accum_out=sum1[:, i:i + 1]).then_inc(s["sum1_ready"], 1)
                    elif name in ("shift1", "shift2"):
                        r = 1 if name == "shift1" else 2
                        act.wait_ge(s["sum1_ready"], b * 2 * CH + CH * r)
                        nc.scalar.activation(log1[:], sum1[:], ACT.Ln).then_inc(s["log1_ready"], 1)
                    elif name == "scoreT":
                        t = take(step)
                        wait_past(act, s["e1l_ready"], b * CH + max(i - STAGE + 1, 0))
                        nc.scalar.activation(e1[:, i % STAGE, :], t[:, :], ACT.Exp).then_inc(s["e1_ready"], 1)
                    elif name == "x2T":
                        t = take(step)
                        wait_past(act, s["acc1_full"], 2 * b)
                        nc.scalar.activation(x2T[:].rearrange("p u c -> p (u c)"), t[:, :],
                                             ACT.Copy).then_inc(s["x2T_ready"], 1)
                    elif name == "xkeep":
                        act.wait_ge(s["x2_ready"], 2 * b + 2)
                        wait_past(act, s["x3s_ready"], 2 * b)
                        nc.scalar.activation(xkeep[:], x2[:], ACT.Identity, scale=keep[:], bias=ngama[:]
                                             ).then_inc(s["xkeep_ready"], 1)
                    elif name == "chan":
                        t = take(step)
                        act.wait_ge(s["nmaxc_ready"], b + 1)
                        nc.scalar.activation(ec[:], t[:, 0:P], ACT.Exp, bias=nmaxc[:], accum_out=sumc[:]
                                             ).then_inc(s["ec_ready"], 1)
                    elif name == "chanT":
                        t = take(step)
                        nc.scalar.activation(ecT[:], t[:, 0:P], ACT.Copy).then_inc(s["ecT_ready"], 1)
                    elif name == "near":
                        t = take(step)
                        act.wait_ge(s["nmax1_ready"], b * (CH + 2) + CH + i + 1)
                        if i == 0:
                            act.wait_ge(s["shf_ready"], 2 * b + 1)
                        for u in range(4 * i, 4 * i + 4):
                            window = t[:, (u % 4) * WPAD:(u % 4) * WPAD + WIN]
                            nc.scalar.activation(window, window, ACT.Exp,
                                                 bias=nmax1[:, u:u + 1], accum_out=sum1[:, u:u + 1]
                                                 ).then_inc(s["sum1_ready"], 1)
                    elif name == "nearT":
                        t = take(step)
                        tv = t[:, :].rearrange("p (u w) -> p u w", w=WPAD)[:, :, 0:WIN]
                        nc.scalar.activation(e2[:, 4 * i:4 * i + 4, :], tv, ACT.Exp).then_inc(s["e2_ready"], 1)
                    elif name == "elu":
                        hc = slice(i * HALF, (i + 1) * HALF)
                        act.wait_ge(s["zneg_ready"], 2 * c + i + 1)
                        nc.scalar.activation(zexp[:, hc], zneg[:, hc], ACT.Exp).then_inc(s["zexp_ready"], 1)

            act.preload_act_table_set("sqrt_and_others")
            for h in range(2):
                hc = slice(h * HALF, (h + 1) * HALF)
                act.wait_ge(s["freq_full"], h + 1)
                nc.scalar.activation(freq[:, hc], acc0[:, hc], ACT.Copy).then_inc(s["freq_ready"], 1)
            act.wait_ge(s["hart_full"], 1)
            nc.scalar.activation(power[:].rearrange("p j m -> p (j m)"), acc1[:, 0:HALF],
                                 ACT.Square).then_inc(s["power_ready"], 1)
            nc.scalar.activation(hart[:].rearrange("p j m -> p (j m)"), acc1[:, 0:HALF],
                                 ACT.Copy).then_inc(s["hart_ready"], 1)
            for part in range(2):
                js = slice(part * CH // 2, (part + 1) * CH // 2)
                act.wait_ge(s["both_ready"], (part + 1) * CH // 2)
                nc.scalar.activation(mag[:, js], both[:, js], ACT.Sqrt, scale=0.5).then_inc(s["mag_ready"], 1)
            act.wait_ge(s["selT_full"], 1)
            nc.scalar.activation(selT[:], acc0[0:NBINS, 0:B], ACT.Copy).then_inc(s["selT_ready"], 1)
            for h in range(2):
                act.wait_ge(s["xe_full"], h + 1)
                hc = slice(h * HALF, (h + 1) * HALF)
                nc.scalar.activation(xe[:, hc], acc0[:, hc], ACT.Copy).then_inc(s["xe_ready"], 1)

        @block.vector
        def _(dve):
            vec = nc.vector
            def fold_bn():
                par = [rp[:, :, i] for i in range(6)]
                dve.wait_ge(s["weights_in"], 16 * 6)
                vec.tensor_scalar(var[:], par[4], EPS, None, ALU.add).then_inc(s["small_dve"], 1)
                dve.wait_ge(s["std_ready"], 1)
                small = [1]

                def link(ins):
                    small[0] += 1
                    ins.then_inc(s["small_dve"], 1)
                    dve.wait_ge(s["small_dve"], small[0])

                link(vec.reciprocal(rstd[:], std[:]))
                link(vec.tensor_tensor(nwt[:], rstd[:], rstd[:], ALU.mult))
                link(vec.tensor_tensor(nwt2[:], nwt[:], var[:], ALU.mult))
                link(vec.tensor_scalar(nwt3[:], nwt2[:], -0.5, 1.5, ALU.mult, ALU.add))
                link(vec.tensor_tensor(rstd2[:], rstd[:], nwt3[:], ALU.mult))
                link(vec.tensor_tensor(scale[:], rstd2[:], par[1], ALU.mult))
                link(vec.tensor_tensor(dev[:], par[0], par[3], ALU.subtract))
                link(vec.tensor_tensor(dev2[:], dev[:], scale[:], ALU.mult))
                link(vec.tensor_tensor(dev3[:], dev2[:], par[2], ALU.add))
                vec.tensor_tensor(bias[:], dev3[:], par[5], ALU.add).then_inc(s["bias_ready"], 1)
                link(vec.tensor_tensor(scale[:, V:V + 1], scale[:, V:V + 1], sc[:, 0:1], ALU.mult))
                link(vec.tensor_tensor(vb[:], dev3[:, V:V + 1], sc[:, 0:1], ALU.mult))
                link(vec.tensor_scalar(keep[:], sc[:, 1:2], -1.0, 1.0, ALU.mult, ALU.add))
                link(vec.tensor_scalar(ngama[:], sc[:, 1:2], -1.0, None, ALU.mult))
                for k in range(3):
                    vec.tensor_scalar(rws[:, k, :], rw[:, k, :], scale[:, k:k + 1], None,
                                      ALU.mult).then_inc(s["wfold_ready"], 1)

            for ph in phases(dve):
                a, b, c = ph.a, ph.b, ph.c

                def take(step):
                    dve.wait_ge(tile_full[ph.slot(step)], ph.filled(step))
                    return slots[ph.slot(step)]

                for step in ph.schedule:
                    name, i = step
                    if name == "bn":
                        fold_bn()
                    elif name == "split":
                        if isinstance(a, int) and a == 0:
                            dve.wait_ge(s["x_first_in"], 16)
                        else:
                            dve.wait_ge(s["x_rest_in"], 16 * (B - 1))
                            dve.wait_ge(s["e0_used"], a * CH)
                        xa = xin[:, a, :]
                        vec.tensor_copy(xh[:], xa).then_inc(s["xh_ready"], 1)
                    elif name == "pool":
                        xa = xin[:, a, :]
                        xv = xa.rearrange("p (y r x c) -> p y x r c", y=POOL, r=H // POOL, x=POOL)
                        vec.tensor_reduce(pooled[:].rearrange("p (y x) -> p y x", y=POOL), xv, AX.XY,
                                          ALU.add).then_inc(s["pooled_ready"], 1)
                    elif name == "gram":
                        t = take(step)
                        vec.tensor_reduce(nmax0[:, i:i + 1], t[:, :], AX.X, ALU.max,
                                          negate=True).then_inc(s["nmax0_ready"], 1)
                    elif name == "norm0":
                        dve.wait_ge(s["e0_ready"], a * CH + i + 1)
                        dve.wait_ge(s["v0_ready"], a + 1)
                        vec.reciprocal(rec0[:, i:i + 1], sum0[:, i:i + 1]).then_inc(s["rec0_ready"], 1)
                        dve.wait_ge(s["rec0_ready"], a * CH + i + 1)
                        vec.tensor_scalar(v0n[:, i, :], v0[:, i, :], rec0[:, i:i + 1], None,
                                          ALU.mult).then_inc(s["v0n_ready"], 1)
                    elif name == "x1":
                        hc = slice(i * HALF, (i + 1) * HALF)
                        dve.wait_ge(s["e0_used"], (a + 1) * CH)
                        vec.tensor_tensor(x1[:, hc], acc0[:, hc], xin[:, a, hc], ALU.add).then_inc(s["x1_ready"], 1)
                    elif name in ("qklow", "aslow"):
                        n = 4 * b + i + (1 if name == "qklow" else 3)
                        hc = slice(i * HALF, (i + 1) * HALF)
                        q, k = slice(0, G), slice(2 * G, 3 * G)
                        dve.wait_ge(s["full_ready"], n)
                        if name == "qklow":
                            wait_past(dve, s["e2_ready"], 2 * b)
                        vec.tensor_copy(qs[0:2 * G, hc], full[0:2 * G, hc]).then_inc(s["qhi_ready"], 1)
                        dve.wait_ge(s["hi_ready"], 2 * n - 1)
                        vec.tensor_tensor(ks[G:2 * G, hc], full[k, hc], ks[k, hc].bitcast(F32), ALU.subtract)
                        dve.wait_ge(s["qhi_ready"], n)
                        vec.tensor_tensor(qs[2 * G:3 * G, hc], full[q, hc], qs[q, hc].bitcast(F32), ALU.subtract
                                          ).then_inc(s["low_ready"], 1)
                    elif name == "val1":
                        t = take(step)
                        dve.wait_ge(s["v1h_ready"], b + 1)
                        vec.tensor_tensor(v1l[:].rearrange("p u c -> p (u c)"), t[:, :],
                                          v1h[:].rearrange("p u c -> p (u c)").bitcast(F32), ALU.subtract
                                          ).then_inc(s["v1_ready"], 1)
                    elif name == "e1h":
                        dve.wait_ge(s["e1_ready"], b * CH + i + 1)
                        wait_past(dve, s["e1_used"], b * CH + max(i - RING + 1, 0))
                        vec.tensor_copy(e1h[:, i % RING, :], e1[:, i % STAGE, :]).then_inc(s["e1h_ready"], 1)
                    elif name == "e1l":
                        dve.wait_ge(s["e1h_ready"], b * CH + i + 1)
                        vec.tensor_tensor(e1l[:, i % RING, :], e1[:, i % STAGE, :],
                                          e1h[:, i % RING, :].bitcast(F32), ALU.subtract).then_inc(s["e1l_ready"], 1)
                    elif name == "score":
                        t = take(step)
                        vec.tensor_reduce(nmax1[:, i:i + 1], t[:, :], AX.X, ALU.max,
                                          negate=True).then_inc(s["nmax1_ready"], 1)
                    elif name in ("shift1", "shift2"):
                        n = 2 * b + (1 if name == "shift1" else 2)
                        dve.wait_ge(s["log1_ready"], n)
                        vec.tensor_tensor(shf[:], nmax1[:], log1[:], ALU.subtract).then_inc(s["shf_ready"], 1)
                        dve.wait_ge(s["shf_ready"], n)
                        vec.tensor_copy(shf_h[:], shf[:]).then_inc(s["shf_h_ready"], 1)
                        dve.wait_ge(s["shf_h_ready"], n)
                        dve.wait_ge(s["diag_zero"], 1)
                        flat = diag[:].rearrange("p u c -> p (u c)")
                        d0 = flat[:, HID:HID + (CH - 1) * (P + 1) + 1:P + 1]
                        d2 = flat[:, 2 * G + HID:2 * G + HID + (CH - 1) * (P + 1) + 1:P + 1]
                        vec.tensor_copy(d0, shf_h[:].bitcast(F32))
                        vec.tensor_tensor(d2, shf[:], shf_h[:].bitcast(F32), ALU.subtract
                                          ).then_inc(s["diag_ready"], 1)
                        t = take(step)
                        vec.tensor_tensor(qs2[:], t[0:KS3, :], qs[:].bitcast(F32), ALU.add
                                          ).then_inc(s["qs2_ready"], 1)
                    elif name == "x2":
                        dve.wait_ge(s["e1_used"], (b + 1) * CH)
                        hc = slice(i * HALF, (i + 1) * HALF)
                        vec.scalar_tensor_tensor(out=x2[:, hc], in0=acc1[:, hc], scalar=vb[:], in1=x1[:, hc],
                                                 op0=ALU.add, op1=ALU.add).then_inc(s["x2_ready"], 1)
                    elif name == "near":
                        t = take(step)
                        tv = t[:, :].rearrange("p (u w) -> p u w", w=WPAD)[:, :, 0:WIN]
                        vec.tensor_reduce(nmax1[:, 4 * i:4 * i + 4], tv, AX.X, ALU.max,
                                          negate=True).then_inc(s["nmax1_ready"], 1)
                    elif name == "chan":
                        t = take(step)
                        vec.tensor_reduce(nmaxc[:], t[:, 0:P], AX.X, ALU.max, negate=True
                                          ).then_inc(s["nmaxc_ready"], 1)
                        dve.wait_ge(s["ec_ready"], b + 1)
                        vec.reciprocal(recc[:], sumc[:]).then_inc(s["recc_ready"], 1)
                        dve.wait_ge(s["recc_ready"], b + 1)
                        vec.tensor_scalar(ecn[:], ec[:], recc[:], None, ALU.mult).then_inc(s["ecn_ready"], 1)
                    elif name == "elu":
                        hc = slice(i * HALF, (i + 1) * HALF)
                        dve.wait_ge(s["acc1_full"], 2 * c + i + 1)
                        vec.tensor_scalar(zneg[:, hc], acc1[:, hc], 0.0, None, ALU.min).then_inc(s["zneg_ready"], 1)
                    elif name == "zelu":
                        hc = slice(i * HALF, (i + 1) * HALF)
                        dve.wait_ge(s["zexp_ready"], 2 * c + i + 1)
                        vec.scalar_tensor_tensor(out=zelu[:, hc], in0=acc1[:, hc], scalar=0.0, in1=zexp[:, hc],
                                                 op0=ALU.max, op1=ALU.add).then_inc(s["zelu_ready"], 1)
                    elif name == "x3":
                        hc = slice(i * HALF, (i + 1) * HALF)
                        dve.wait_ge(s["zelu_ready"], 2 * c + i + 1)
                        dve.wait_ge(s["xkeep_ready"], c + 1)
                        if a is None:
                            dve.wait_ge(s["x3_ready"], c)
                        else:
                            dve.wait_ge(s["xl_ready"], a + 1)
                        vec.scalar_tensor_tensor(out=x3s[:, hc], in0=zelu[:, hc], scalar=sc[:, 1:2], in1=xkeep[:, hc],
                                                 op0=ALU.mult, op1=ALU.add).then_inc(s["x3s_ready"], 1)
                    elif name == "xproj":
                        dve.wait_ge(s["xproj_full"], c + 1)
                        at = slice(c * M, (c + 1) * M) if isinstance(c, int) else bass.ds(c * M, M)
                        t = acc0[:, 0:CH * M].rearrange("p (u m) -> p u m", m=M)
                        vec.tensor_copy(xp[:, :, 0, at], t).then_inc(s["xp_h_ready"], 1)
                        dve.wait_ge(s["xp_h_ready"], c + 1)
                        vec.tensor_tensor(xp[:, :, 1, at], t, xp[:, :, 0, at].bitcast(F32), ALU.subtract
                                          ).then_inc(s["xp_ready"], 1)

            dve.wait_ge(s["flip_full"], 1)
            dve.wait_ge(s["power_ready"], 1)
            for j in range(CH):
                o = (CH - j) % CH * BM
                vec.tensor_tensor(both[:, j, :], acc0[:, o:o + BM], power[:, j, :], ALU.add).then_inc(s["both_ready"], 1)
            for part in range(2):
                js = slice(part * CH // 2, (part + 1) * CH // 2)
                dve.wait_ge(s["mag_ready"], part + 1)
                vec.tensor_reduce(msum[:, js].rearrange("p j b -> p (j b)"),
                                  mag[:, js].rearrange("p j (b m) -> p (j b) m", m=M),
                                  AX.X, ALU.add).then_inc(s["msum_ready"], 1)
            count = [0]

            def step(ins):
                count[0] += 1
                ins.then_inc(s["pick"], 1)
                dve.wait_ge(s["pick"], count[0])

            NB = NBINS
            e, mean = es[:, 1:NB + 1], es[:, NB + 2:NB + 3]
            top, none, e_max, low, low2, top2, first, two = (one[:, k:k + 1] for k in range(8))
            dve.wait_ge(s["energy_full"], 1)
            step(vec.tensor_copy(es[:], acc0[0:B, HALF:HALF + NB + 3]))
            step(vec.scalar_tensor_tensor(out=pk[0][:], in0=es[:, 0:NB], scalar=mean, in1=es[:, 2:NB + 2],
                                          op0=ALU.max, op1=ALU.max))
            step(vec.tensor_tensor(pk[1][:], e, pk[0][:], ALU.is_gt))
            step(vec.tensor_tensor(pk[2][:], pk[1][:], e, ALU.mult))
            vec.tensor_reduce(e_max, e, AX.X, ALU.max)
            step(vec.tensor_reduce(top, pk[2][:], AX.X, ALU.max))
            step(vec.tensor_scalar(none, top, 0.0, None, ALU.is_equal))
            vec.scalar_tensor_tensor(out=first, in0=e_max, scalar=none, in1=top, op0=ALU.mult, op1=ALU.add)
            step(vec.scalar_tensor_tensor(out=pk[3][:], in0=e, scalar=none, in1=pk[2][:],
                                          op0=ALU.mult, op1=ALU.max))
            dve.wait_ge(s["masks_ready"], 6)

            def lowest(vals, top, key, low):
                step(vec.scalar_tensor_tensor(out=key, in0=vals, scalar=top, in1=ramp[:],
                                              op0=ALU.is_equal, op1=ALU.mult))
                step(vec.tensor_reduce(low, key, AX.X, ALU.min))

            lowest(pk[3][:], first, sel[0][:], low)
            step(vec.scalar_tensor_tensor(out=sel[1][:], in0=ramp[:], scalar=low, in1=pk[2][:],
                                          op0=ALU.not_equal, op1=ALU.mult))
            step(vec.tensor_reduce(top2, sel[1][:], AX.X, ALU.max))
            lowest(sel[1][:], top2, sel[2][:], low2)
            vec.tensor_scalar(sel[3][:], ramp[:], low, None, ALU.is_equal)
            vec.tensor_scalar(two, top2, 0.0, None, ALU.is_gt)
            step(vec.tensor_scalar(sel[4][:], ramp[:], low2, None, ALU.is_equal))
            vec.scalar_tensor_tensor(out=sel[5][:], in0=sel[4][:], scalar=two, in1=sel[3][:],
                                     op0=ALU.mult, op1=ALU.add).then_inc(s["sel_ready"], 1)
            dve.wait_ge(s["enh_full"], 1)
            vec.tensor_scalar(enh[:].rearrange("p s j b -> p (s j b)"), acc1[:, HALF:HALF + 2 * CH * B],
                              1.0, None, ALU.min).then_inc(s["enh_chain"], 1)
            dve.wait_ge(s["enh_chain"], 1)
            vec.tensor_tensor(enh2[:], enh[:, 0], enh[:, 1], ALU.add).then_inc(s["enh_chain"], 1)
            dve.wait_ge(s["enh_chain"], 2)
            vec.tensor_tensor(gain[:], enh2[:], gains[:, :, 1:2].to_broadcast([P, CH, B]), ALU.mult
                              ).then_inc(s["enh_chain"], 1)
            dve.wait_ge(s["enh_chain"], 3)
            vec.tensor_tensor(enh2[:], gain[:], gains[:, :, 0:1].to_broadcast([P, CH, B]), ALU.add
                              ).then_inc(s["enh_chain"], 1)
            dve.wait_ge(s["enh_chain"], 4)
            dve.wait_ge(s["hart_ready"], 1)
            for part in range(2):
                js = slice(part * CH // 2, (part + 1) * CH // 2)
                gb = enh2[:, js].rearrange("p j b -> p (j b)").unsqueeze(2).to_broadcast([P, CH // 2 * B, M])
                vec.tensor_tensor(coef[:, js].rearrange("p j (b m) -> p (j b) m", m=M),
                                  hart[:, js].rearrange("p j (b m) -> p (j b) m", m=M), gb, ALU.mult
                                  ).then_inc(s["enh_chain"], 1)
                dve.wait_ge(s["enh_chain"], 5 + 2 * part)
                vec.tensor_copy(coef2[:, js, 0, :], coef[:, js]).then_inc(s["enh_chain"], 1)
                dve.wait_ge(s["enh_chain"], 6 + 2 * part)
                vec.tensor_tensor(coef2[:, js, 1, :], coef[:, js], coef2[:, js, 0, :].bitcast(F32), ALU.subtract
                                  ).then_inc(s["coef_ready"], 1)
            for b in range(B):
                t = (acc1, tile[0], tile[1], acc0)[b]
                for h in range(2):
                    hc = slice(h * HALF, (h + 1) * HALF)
                    dve.wait_ge(s["y_full"], 2 * b + h + 1)
                    dve.wait_ge(s["x3_ready"], B)
                    vec.tensor_tensor(yout[:, b, hc], t[:, hc], x3[:, b, hc], ALU.add).then_inc(s["y_ready"], 1)

        @block.gpsimd
        def _(pool):
            gp = nc.gpsimd
            gp.memset(diag[:], 0.0).then_inc(s["diag_zero"], 1)
            def constants():
                pool.wait_ge(s["weights_in"], 16 * 6)
                pool.wait_ge(s["const_in"], 16 * 3)
                gp.tensor_copy(identb[:], ident[:]).then_inc(s["masks_ready"], 1)
                gp.tensor_copy(nearb[:], near).then_inc(s["masks_ready"], 1)
                gp.tensor_copy(chainb[:], chain[:]).then_inc(s["masks_ready"], 1)
                for side in range(2):
                    pool.wait_ge(s["region_in"], 16 * (side + 1))
                    gp.tensor_copy(regionb[:, side], region).then_inc(s["masks_ready"], 1)
                gp.iota(ramp[:], pattern=[[1, NBINS]], base=-NBINS, channel_multiplier=0,
                        allow_small_or_imprecise_dtypes=True).then_inc(s["masks_ready"], 1)

            for ph in phases(pool):
                b, c = ph.b, ph.c
                for step in ph.schedule:
                    name, i = step
                    if name == "split":
                        pool.wait_ge(s["xh_ready"], ph.a + 1)
                        gp.tensor_tensor(xl[:], xin[:, ph.a, :], xh[:].bitcast(F32), ALU.subtract
                                         ).then_inc(s["xl_ready"], 1)
                    elif name == "fold":
                        constants()
                    elif step == ("qkproj", 0) and ph.a is None:
                        pool.wait_ge(s["x1_ready"], 2 * B)
                        for j in range(CH):
                            gp.dma_start(cas_h[:, j, :], cas_h_in[:, j, :]).then_inc(s["cas_h_in"], 16)
                            gp.dma_start(cas_l[:, j, :], cas_l_in[:, j, :]).then_inc(s["cas_l_in"], 16)
                    elif step == ("x3", 1):
                        pool.wait_ge(s["x3s_ready"], 2 * c + 2)
                        gp.tensor_copy(x3[:, c, :], x3s[:]).then_inc(s["x3_ready"], 1)

def _tables():
    f = np.float32
    idx = np.arange(N)
    kh, kw = idx // W, idx % W
    turn = (np.outer(kh, kh) + np.outer(kw, kw)) % H
    ang = 2 * np.pi * np.arange(H) / H
    cas = ((np.cos(ang) + np.sin(ang)) / H)[turn].astype(f)
    order = idx.reshape(P, CH).T
    cas = np.ascontiguousarray(cas[order].transpose(1, 0, 2))
    def high_part(v):
        return (v.view(np.uint32) & np.uint32(0xFFFFF000)).view(f)

    cas_h = high_part(cas)
    cas_l = high_part(cas - cas_h)
    neg = ((-kh) % H) * W + (-kw) % W
    where = np.empty(N, int)
    where[order.ravel()] = np.arange(N) % P
    flip = np.zeros((P, 2, P), f)
    for kind, j in ((0, 0), (1, 1)):
        for p in range(P):
            flip[where[neg[order[j, p]]], kind, p] = 1
    pi = f(np.pi)
    y, xx = ((kh + H // 2) % H).astype(f), ((kw + W // 2) % W).astype(f)
    r = np.sqrt((y - H // 2) ** 2 + (xx - W // 2) ** 2)
    theta = (np.arctan2((y - f(H // 2)).astype(float), xx - f(W // 2)).astype(f) + pi).astype(f)
    high = (r > f(0.3 * (H // 2))).astype(f)
    edges = _edges()
    mod = np.mod(theta, pi).astype(f)
    bin_of = np.clip(np.searchsorted(edges, mod, side="left") - 1, 0, NBINS - 1)
    onehot = np.zeros((N, NBINS), f)
    onehot[idx, bin_of] = high
    pad = np.pad(onehot, ((0, 0), (1, 1)))
    smooth = pad[:, :-2] + 2 * pad[:, 1:-1] + pad[:, 2:]
    smooth = np.concatenate([smooth[:, -1:], smooth, smooth[:, :1], smooth.sum(1, keepdims=True) / f(NBINS)], 1)
    bins = np.ascontiguousarray(smooth[order].transpose(1, 0, 2))
    centre = ((edges[:-1] + edges[1:]) * f(0.5)).astype(f)
    diff = np.abs(theta[None] - centre[:, None])
    diff = np.minimum(diff, pi - diff)
    inside = ((diff <= f(np.radians(15.0))) & (high[None] > 0)).astype(f)
    region = np.stack([inside[:, order], inside[:, neg[order]]], 1)
    assert (high == high[neg]).all()
    gains = np.stack([np.where(high > 0, f(0.8), f(1.0)), f(0.2) * high], -1).astype(f)[order].transpose(1, 0, 2)
    n, m = np.arange(P), np.arange(WIN)
    di = np.abs((n // W + 1)[:, None] - (m // W)[None])
    dj = np.abs((n % W)[:, None] - (m % W)[None])
    adj = (di <= 1) & (dj <= 1) & ~((di == 0) & (dj == 0))
    near = np.full((P, 3, WIN), -9e15, f)
    for kind, ok in enumerate((m >= 0, m >= W, m < WIN - W)):
        near[:, kind][adj & ok[None]] = 0
    c = np.arange(C)
    chain = np.where(np.abs(c[:, None] - c[None]) == 1, f(0), f(-9e15)).astype(f)
    return dict(ident_in=np.eye(P, dtype=f), near_in=near, chain_in=chain, flip_in=flip, cas_h_in=cas_h, cas_l_in=cas_l,
                fold_in=np.concatenate([np.eye(BM, dtype=f)] * 2), bins_in=bins,
                region_in=np.ascontiguousarray(region), gains_in=np.ascontiguousarray(gains))


def _edges():
    f = np.float32
    inner = np.arange(NBINS, dtype=f) * (f(1) / f(NBINS) * f(np.pi))
    return np.concatenate([inner, np.array([np.pi], f)])


def _pack(i):
    f = np.float32
    rows_w, rows_p = np.zeros((P, 3, P), f), np.zeros((P, 3, 6), f)
    rows_w[:, V] = i["L1_conv_v_w"]
    for n, part in enumerate(("b", "g", "beta", "mean", "var")):
        rows_p[:, V, n] = i["L1_conv_v_" + part]
    for g in range(4):
        at = slice(g * G, g * G + HID)
        pre = "L1_conv_q_" if g < 2 else "L1_conv_k_"
        rows_w[at, QK] = i[pre + "w"]
        for n, part in enumerate(("b", "g", "beta", "mean", "var")):
            rows_p[at, QK, n] = i[pre + part]
        t = "a" if g < 2 else "s"
        rows_w[at, AS] = i[f"L2_conv_w{t}"]
        for n, part in ((1, "g"), (2, "b"), (3, "m"), (4, "v")):
            rows_p[at, AS, n] = i[f"L2_conv_{part}{t}"]
        if g >= 2:
            rows_p[g * G + HID:g * G + HID + CH, :V, 5] = 1
    return rows_w, rows_p


def kernel(**inputs):
    import numpy as _np
    import concourse.bacc as _bacc
    from concourse import mybir as _mybir
    from concourse.bass_utils import run_bass_kernel_spmd as _run

    i = {k: _np.asarray(v) for k, v in inputs.items()}
    rows_w, rows_p = _pack(i)
    wout = _np.zeros((2, BM, B, P), _np.float32)
    for b in range(B):
        wout[:, b * M:(b + 1) * M, b] = i["L3_conv_w_out"].T
    wout = wout.reshape(2 * BM, B, P)
    scal = _np.zeros((P, 2), _np.float32)
    scal[:, 0] = i["L1_conv_gamma"][0]
    scal[:, 1] = i["L2_conv_gama"][0]
    data = dict(x=i["x"].reshape(B, C, N), rows_w=rows_w, rows_p=rows_p, scal=scal, wg_t=i["L0_conv_w_gap"].T,
                w_conv=i["L0_conv_w_conv"], win_t=i["L3_conv_w_in"].T, wout_t=wout, **_tables())
    nc = _bacc.Bacc("TRN2", target_bir_lowering=False, num_devices=1)
    arrays, args = {}, {}
    for name, v in data.items():
        v = _np.ascontiguousarray(v)
        arrays["in_" + name] = v
        args[name] = nc.dram_tensor("in_" + name, v.shape, _mybir.dt.from_np(v.dtype), kind="ExternalInput").ap()
    args["out"] = nc.dram_tensor("out_0", (B, C, N), _mybir.dt.float32, kind="ExternalOutput").ap()
    conv_seq(nc, **args)
    r = _run(nc, [arrays], core_ids=[0])
    return r.results[0]["out_0"].reshape(B, C, H, W)
```
